# Optimizing a Trainium2 kernel written in Bass

```python
import numpy as np
import jax
import jax.numpy as jnp

def _softmax(x, axis=-1):
    return jax.nn.softmax(x, axis=axis)

def _gelu(x):
    return jax.nn.gelu(x, approximate=True)

def _silu(x):
    return jax.nn.silu(x)

def _sigmoid(x):
    return jax.nn.sigmoid(x)

def _layernorm(x, axis=-1, eps=1e-05):
    m = jnp.mean(x, axis=axis, keepdims=True)
    v = jnp.var(x, axis=axis, keepdims=True)
    return (x - m) / jnp.sqrt(v + eps)

def _scatter_add(tgt, idx, src, axis=0):
    return tgt.at[idx].add(src)

def _segment_sum(src, seg, n):
    return jax.ops.segment_sum(src, seg, n)
kernel_name = 'mk_perceiver_d1_seqx_r8_818b73'

def setup_inputs(seed: int=0):
    np.random.seed(seed)
    _w = jnp.asarray

    def _rec_inputs():
        import jax
        import jax.numpy as jnp
        _rk = jax.random.key(seed)
        x = -1.394e-06 + 0.9999 * jax.random.normal(jax.random.fold_in(_rk, 1), (4, 128, 128), jnp.float32)
        _lenS = 128 - jax.random.randint(jax.random.fold_in(_rk, 7), (4,), 0, max(1, 128 // 4) + 1, jnp.int32)
        _lenS2 = 2048 - jax.random.randint(jax.random.fold_in(_rk, 8), (4,), 0, max(1, 2048 // 4) + 1, jnp.int32)
        _ctx_1024P = jax.random.normal(jax.random.fold_in(_rk, 11), (4, 16, 128), jnp.float32)
        _ctx_1024c = jax.random.dirichlet(jax.random.fold_in(_rk, 511), 0.3 * jnp.ones((16,), jnp.float32), (4, 2048))
        _ctx_1024t = jnp.einsum('bsk,bkd->bsd', _ctx_1024c, _ctx_1024P)
        _ctx_1024t = _ctx_1024t * jax.lax.rsqrt(jnp.mean(jnp.square(_ctx_1024t)) + 1e-12) * 0.953939
        ctx_1024 = -0.000392918 + 0.999932 * (_ctx_1024t + 0.3 * jax.random.normal(jax.random.fold_in(_rk, 611), (4, 2048, 128), jnp.float32))
        _validS = jnp.arange(128)[None, :] < _lenS[:, None]
        _validS2 = jnp.arange(2048)[None, :] < _lenS2[:, None]
        _causal = jnp.tril(jnp.ones((128, 128), dtype=bool))
        mask_BxS2_bk0 = jnp.logical_not(jnp.broadcast_to(_validS2[:, :], (4, 2048)))
        return (x, ctx_1024, mask_BxS2_bk0)
    x, ctx_1024, mask_BxS2_bk0 = _rec_inputs()

    def _L0_xattn_setup():
        import jax, jax.numpy as jnp
        import numpy as np
        DIM = 128
        DIM_LATENT = 128
        DIM_HEAD = 64
        INNER = max(DIM, DIM_LATENT)
        HEADS = INNER // DIM_HEAD
        SCALE = DIM_HEAD ** (-0.5)
        LN_EPS = 1e-05
        RMS_EPS = 1e-08

        def layernorm(x, g, b):
            mu = jnp.mean(x, axis=-1, keepdims=True)
            var = jnp.mean(jnp.square(x - mu), axis=-1, keepdims=True)
            return (x - mu) * jax.lax.rsqrt(var + LN_EPS) * g + b

        def rmsnorm(x, gamma):
            n = jnp.linalg.norm(x, axis=-1, keepdims=True) * x.shape[-1] ** (-0.5)
            return x / jnp.maximum(n, RMS_EPS) * gamma
        key = jax.random.key(seed)
        ks = jax.random.split(key, 8)
        b, n, nl = (8, 256, 64)
        x = jax.random.normal(ks[0], (b, n, DIM), dtype=jnp.float32)
        latents = jax.random.normal(ks[1], (b, nl, DIM_LATENT), dtype=jnp.float32)
        mask = jax.random.randint(ks[2], (b, n), 0, 2).astype(bool)
        init = lambda k, shape, fan_in: jax.random.normal(k, shape, jnp.float32) * fan_in ** (-0.5)
        return {'x': x, 'latents': latents, 'mask': mask, 'ln_x_g': jnp.ones((DIM,), jnp.float32), 'ln_x_b': jnp.zeros((DIM,), jnp.float32), 'ln_l_g': jnp.ones((DIM_LATENT,), jnp.float32), 'ln_l_b': jnp.zeros((DIM_LATENT,), jnp.float32), 'q_gamma': jnp.ones((DIM_HEAD,), jnp.float32), 'k_gamma': jnp.ones((DIM_HEAD,), jnp.float32), 'W_q': init(ks[3], (DIM_LATENT, INNER), DIM_LATENT), 'W_kv': init(ks[4], (DIM, 2 * INNER), DIM), 'W_out': init(ks[5], (INNER, DIM_LATENT), INNER), 'b_out': jnp.zeros((DIM_LATENT,), jnp.float32)}
    _L0_xattn_all = _L0_xattn_setup()
    _L0_xattn_in = {k: v for k, v in _L0_xattn_all.items() if k in ('ln_x_g', 'ln_x_b', 'ln_l_g', 'ln_l_b', 'q_gamma', 'k_gamma', 'W_q', 'W_kv', 'W_out', 'b_out')}
    del _L0_xattn_all

    def _L0_attn_setup():
        import jax, jax.numpy as jnp
        import numpy as np
        DECAY = 0.99
        LR = 0.01

        def _reference_tuple_inner(x, Wk, bk, Wv, bv, Wq, bq, Wo, bo):
            B, S, D = x.shape
            M = Wk.shape[0]
            k = jnp.einsum('bsd,md->bsm', x, Wk) + bk
            v = jnp.einsum('bsd,md->bsm', x, Wv) + bv
            q = jnp.einsum('bsd,md->bsm', x, Wq) + bq

            def step(state, kvq):
                k_t, v_t, q_t = kvq
                out_t = jnp.einsum('bij,bj->bi', state, q_t)
                state = DECAY * state + LR * jnp.einsum('bi,bj->bij', v_t, k_t)
                return (state, out_t)
            state0 = jnp.zeros((B, M, M), x.dtype)
            xs = (jnp.swapaxes(k, 0, 1), jnp.swapaxes(v, 0, 1), jnp.swapaxes(q, 0, 1))
            state, outs = jax.lax.scan(step, state0, xs)
            outs = jnp.swapaxes(outs, 0, 1)
            y = jnp.einsum('bsm,dm->bsd', outs, Wo) + bo
            return (y, state)
        key = jax.random.key(seed)
        ks = jax.random.split(key, 6)
        B, S, D, M = (4, 512, 128, 128)
        sD = 1.0 / np.sqrt(D)
        sM = 1.0 / np.sqrt(M)
        return {'x': jax.random.normal(ks[0], (B, S, D), dtype=jnp.float32), 'Wk': jax.random.uniform(ks[1], (M, D), jnp.float32, -sD, sD), 'bk': jnp.zeros((M,), jnp.float32), 'Wv': jax.random.uniform(ks[2], (M, D), jnp.float32, -sD, sD), 'bv': jnp.zeros((M,), jnp.float32), 'Wq': jax.random.uniform(ks[3], (M, D), jnp.float32, -sD, sD), 'bq': jnp.zeros((M,), jnp.float32), 'Wo': jax.random.uniform(ks[4], (D, M), jnp.float32, -sM, sM), 'bo': jnp.zeros((D,), jnp.float32)}
    _L0_attn_all = _L0_attn_setup()
    _L0_attn_in = {k: v for k, v in _L0_attn_all.items() if k in ('Wk', 'bk', 'Wv', 'bv', 'Wq', 'bq', 'Wo', 'bo')}
    del _L0_attn_all

    def _L0_ffn_setup():
        import jax, jax.numpy as jnp
        import numpy as np
        D_MODEL = 128
        N_EXPERTS = 8
        TOP_K = 2
        B, S = (4, 256)
        key = jax.random.key(seed)
        k_x, k_g, k_w = jax.random.split(key, 3)
        x = jax.random.normal(k_x, (B, S, D_MODEL), dtype=jnp.float32)
        gate_w = jax.random.normal(k_g, (N_EXPERTS, D_MODEL), dtype=jnp.float32) * (1.0 / np.sqrt(D_MODEL))
        bound = float(np.sqrt(6.0 / (D_MODEL + D_MODEL)))
        weight = jax.random.uniform(k_w, (N_EXPERTS, D_MODEL, D_MODEL), dtype=jnp.float32, minval=-bound, maxval=bound)
        return {'x': x, 'gate_w': gate_w, 'weight': weight}
    _L0_ffn_all = _L0_ffn_setup()
    _L0_ffn_in = {k: v for k, v in _L0_ffn_all.items() if k in ('gate_w', 'weight')}
    del _L0_ffn_all
    return {'x': x, 'ctx_1024': ctx_1024, 'mask_BxS2_bk0': mask_BxS2_bk0, 'L0_xattn_ln_x_g': _L0_xattn_in['ln_x_g'], 'L0_xattn_ln_x_b': _L0_xattn_in['ln_x_b'], 'L0_xattn_ln_l_g': _L0_xattn_in['ln_l_g'], 'L0_xattn_ln_l_b': _L0_xattn_in['ln_l_b'], 'L0_xattn_q_gamma': _L0_xattn_in['q_gamma'], 'L0_xattn_k_gamma': _L0_xattn_in['k_gamma'], 'L0_xattn_W_q': _L0_xattn_in['W_q'], 'L0_xattn_W_kv': _L0_xattn_in['W_kv'], 'L0_xattn_W_out': _L0_xattn_in['W_out'], 'L0_xattn_b_out': _L0_xattn_in['b_out'], 'L0_attn_Wk': _L0_attn_in['Wk'], 'L0_attn_bk': _L0_attn_in['bk'], 'L0_attn_Wv': _L0_attn_in['Wv'], 'L0_attn_bv': _L0_attn_in['bv'], 'L0_attn_Wq': _L0_attn_in['Wq'], 'L0_attn_bq': _L0_attn_in['bq'], 'L0_attn_Wo': _L0_attn_in['Wo'], 'L0_attn_bo': _L0_attn_in['bo'], 'L0_ffn_gate_w': _L0_ffn_in['gate_w'], 'L0_ffn_weight': _L0_ffn_in['weight']}

def reference(x, ctx_1024, mask_BxS2_bk0, L0_xattn_ln_x_g, L0_xattn_ln_x_b, L0_xattn_ln_l_g, L0_xattn_ln_l_b, L0_xattn_q_gamma, L0_xattn_k_gamma, L0_xattn_W_q, L0_xattn_W_kv, L0_xattn_W_out, L0_xattn_b_out, L0_attn_Wk, L0_attn_bk, L0_attn_Wv, L0_attn_bv, L0_attn_Wq, L0_attn_bq, L0_attn_Wo, L0_attn_bo, L0_ffn_gate_w, L0_ffn_weight):
    import jax
    import jax.numpy as jnp

    def _L0_xattn_ref(x, latents, mask, ln_x_g, ln_x_b, ln_l_g, ln_l_b, q_gamma, k_gamma, W_q, W_kv, W_out, b_out):
        import jax, jax.numpy as jnp
        import numpy as np
        DIM = 128
        DIM_LATENT = 128
        DIM_HEAD = 64
        INNER = max(DIM, DIM_LATENT)
        HEADS = INNER // DIM_HEAD
        SCALE = DIM_HEAD ** (-0.5)
        LN_EPS = 1e-05
        RMS_EPS = 1e-08

        def layernorm(x, g, b):
            mu = jnp.mean(x, axis=-1, keepdims=True)
            var = jnp.mean(jnp.square(x - mu), axis=-1, keepdims=True)
            return (x - mu) * jax.lax.rsqrt(var + LN_EPS) * g + b

        def rmsnorm(x, gamma):
            n = jnp.linalg.norm(x, axis=-1, keepdims=True) * x.shape[-1] ** (-0.5)
            return x / jnp.maximum(n, RMS_EPS) * gamma
        b, n, _ = x.shape
        nl = latents.shape[1]
        xn = layernorm(x, ln_x_g, ln_x_b)
        ln = layernorm(latents, ln_l_g, ln_l_b)
        q = ln @ W_q
        kv = jnp.concatenate([xn @ W_kv, ln @ W_kv], axis=1)
        k, v = (kv[..., :INNER], kv[..., INNER:])
        to_heads = lambda t: t.reshape(t.shape[0], t.shape[1], HEADS, DIM_HEAD).transpose(0, 2, 1, 3)
        q, k, v = (to_heads(q), to_heads(k), to_heads(v))
        qn = rmsnorm(q, q_gamma) * SCALE
        kn = rmsnorm(k, k_gamma)
        sim = jnp.einsum('bhid,bhjd->bhij', qn, kn)
        full_mask = jnp.pad(mask, ((0, 0), (0, nl)), constant_values=True)
        neg = -jnp.finfo(sim.dtype).max
        sim = jnp.where(full_mask[:, None, None, :], sim, neg)
        attn = jax.nn.softmax(sim.astype(jnp.float32), axis=-1).astype(sim.dtype)
        out = jnp.einsum('bhij,bhjd->bhid', attn, v)
        out = out.transpose(0, 2, 1, 3).reshape(b, nl, INNER)
        return out @ W_out + b_out

    def _L0_attn_ref(x, Wk, bk, Wv, bv, Wq, bq, Wo, bo):
        import jax, jax.numpy as jnp
        import numpy as np
        DECAY = 0.99
        LR = 0.01

        def _reference_tuple_inner(x, Wk, bk, Wv, bv, Wq, bq, Wo, bo):
            B, S, D = x.shape
            M = Wk.shape[0]
            k = jnp.einsum('bsd,md->bsm', x, Wk) + bk
            v = jnp.einsum('bsd,md->bsm', x, Wv) + bv
            q = jnp.einsum('bsd,md->bsm', x, Wq) + bq

            def step(state, kvq):
                k_t, v_t, q_t = kvq
                out_t = jnp.einsum('bij,bj->bi', state, q_t)
                state = DECAY * state + LR * jnp.einsum('bi,bj->bij', v_t, k_t)
                return (state, out_t)
            state0 = jnp.zeros((B, M, M), x.dtype)
            xs = (jnp.swapaxes(k, 0, 1), jnp.swapaxes(v, 0, 1), jnp.swapaxes(q, 0, 1))
            state, outs = jax.lax.scan(step, state0, xs)
            outs = jnp.swapaxes(outs, 0, 1)
            y = jnp.einsum('bsm,dm->bsd', outs, Wo) + bo
            return (y, state)
        return _reference_tuple_inner(x, Wk, bk, Wv, bv, Wq, bq, Wo, bo)[0]

    def _L0_ffn_ref(x, gate_w, weight):
        import jax, jax.numpy as jnp
        import numpy as np
        D_MODEL = 128
        N_EXPERTS = 8
        TOP_K = 2
        B, S = (4, 256)
        logits = jnp.einsum('bsd,ed->bse', x, gate_w)
        topk_vals, topk_idx = jax.lax.top_k(logits, TOP_K)
        topk_weights = jax.nn.softmax(topk_vals, axis=-1)
        one_hot = jax.nn.one_hot(topk_idx, N_EXPERTS, dtype=x.dtype)
        weights_full = jnp.einsum('bsk,bske->bse', topk_weights, one_hot)
        expert_out = jnp.einsum('bsd,edh->bseh', x, weight)
        out = jnp.einsum('bse,bseh->bsh', weights_full, expert_out)
        return out
    x = x + _L0_xattn_ref(ctx_1024, _layernorm(x, axis=-1), mask_BxS2_bk0, L0_xattn_ln_x_g, L0_xattn_ln_x_b, L0_xattn_ln_l_g, L0_xattn_ln_l_b, L0_xattn_q_gamma, L0_xattn_k_gamma, L0_xattn_W_q, L0_xattn_W_kv, L0_xattn_W_out, L0_xattn_b_out)
    x = x + _L0_attn_ref(_layernorm(x, axis=-1), L0_attn_Wk, L0_attn_bk, L0_attn_Wv, L0_attn_bv, L0_attn_Wq, L0_attn_bq, L0_attn_Wo, L0_attn_bo)
    x = x + _L0_ffn_ref(_layernorm(x, axis=-1), L0_ffn_gate_w, L0_ffn_weight)
    return x

_drawn_inputs = setup_inputs


def setup_inputs(seed=0):
    import zlib

    import numpy as np

    out = dict(_drawn_inputs(seed))
    spreads = {'L0_xattn_ln_x_g': (1.0, 0.2),
     'L0_xattn_ln_x_b': (0.0, 0.1),
     'L0_xattn_ln_l_g': (1.0, 0.2),
     'L0_xattn_ln_l_b': (0.0, 0.1),
     'L0_xattn_q_gamma': (1.0, 0.2),
     'L0_xattn_k_gamma': (1.0, 0.2),
     'L0_xattn_b_out': (0.0, 0.1),
     'L0_attn_bk': (0.0, 0.1),
     'L0_attn_bv': (0.0, 0.1),
     'L0_attn_bq': (0.0, 0.1),
     'L0_attn_bo': (0.0, 0.1)}
    factors = {}
    for name, (base, spread) in spreads.items():
        noise = np.random.default_rng([zlib.crc32(name.encode()), seed]).standard_normal(out[name].shape)
        drawn = base * np.exp(spread * noise) if base else spread * noise
        out[name] = jnp.asarray(drawn.astype(out[name].dtype))
    for name, factor in factors.items():
        out[name] = (out[name] * factor).astype(out[name].dtype)
    return out
```

```python
from contextlib import ExitStack

import concourse.bass as bass
import numpy as np
from concourse import mybir

ALU = mybir.AluOpType
ACT = mybir.ActivationFunctionType
F32 = mybir.dt.float32
U8 = mybir.dt.uint8
U32 = mybir.dt.uint32
AX = mybir.AxisListType

P = 128
B = 4
S2 = 2048
H = 2
DH = P // H
E = 8
TG = 4
TPB = S2 // P
GPB = TPB // TG
NG = B * GPB
LN_EPS = 1e-5
SSQ_MIN = DH * 1e-16
DECAY, LR = 0.99, 0.01

FIRST = dict(g_l=(0, 1), b_l=(1, 2), g_x=(2, 3), b_x=(3, 4), ident=(4, 132), cent=(132, 260), wq=(260, 388),
             wk=(388, 516), wv=(516, 644), wout=(644, 772))
LATER = dict(decay=(0, 128), wkT=(128, 256), wvT=(256, 384), wqT=(384, 512), woT=(512, 640), gate=(640, 648))
ROWS = dict(bk=(0, 128), bv=(128, 256), bq=(256, 384), e_last=(384, 512))
BCAST = dict(b_out=(0, 128), b_o=(128, 256), q_gamma=(256, 320), k_gamma=(320, 384), iota=(384, 392))


def build(nc, x, ctx_x, mask, first, later, rows, bcast, experts, out):
    ctx = ExitStack()
    with ctx:
        def sb(name, shape, dt=F32):
            return ctx.enter_context(nc.sbuf_tensor(name, shape, dt))

        def ps(name, shape):
            return ctx.enter_context(nc.psum_tensor(name, shape, F32))

        def sem(name):
            return ctx.enter_context(nc.semaphore(name))

        w1 = sb("w1", [P, 772])
        w2 = sb("w2", [P, 648])
        w1_ = {k: w1[:, a:z] for k, (a, z) in FIRST.items()}
        w2_ = {k: w2[:, a:z] for k, (a, z) in LATER.items()}
        row = sb("row", [1, 512])
        row_ = {k: row[:, a:z] for k, (a, z) in ROWS.items()}
        bc = sb("bc", [P, 392])
        bc_ = {k: bc[:, a:z] for k, (a, z) in BCAST.items()}
        ident = w1_["ident"]
        wexp = sb("wexp", [P, E, P])
        mask8 = sb("mask8", [P, B, TPB], U8)
        maskf = sb("maskf", [P, B, TPB])

        xin = sb("xin", [P, B, P])
        xres = sb("xres", [P, B, P])
        xmid = sb("xmid", [P, B, P])
        xctx = sb("xctx", [P, GPB, TG, P])
        zt = sb("zt", [P, GPB, TG, P])
        zT = sb("zT", [P, 2, TG, P])
        ksq = sb("ksq", [P, TG * P])
        sims = sb("sims", [P, 2, TG * H, P])
        prob = sb("prob", [P, GPB, TG, H * P])

        amat = sb("amat", [P, 2, P])
        wproj = sb("wproj", [P, 3, P])
        wT = sb("wT", [P, 2, 2, P])
        vo = sb("vo", [P, 2, H, P + 1])
        gam = sb("gam", [P, H, DH])
        zl = sb("zl", [P, B, P])
        zlT = sb("zlT", [P, B, P])
        qksq = sb("qksq", [P, 2, B * P])
        qn = sb("qn", [P, B * H, DH])
        qg = sb("qg", [P, B, P])
        qT = sb("qT", [P, B, P])
        qw = sb("qw", [P, 2, B, H, P])
        siml = sb("siml", [P, B * H, P])
        probl = sb("probl", [P, B, H * P])
        y = sb("y", [P, 2, B, H, P])

        bst = sb("bst", [P, TG, 6])
        stt = sb("stt", [P, 6, TG])
        nb = sb("nb", [P, 12])
        nl = sb("nl", [P, 12])
        ny = sb("ny", [P, 12])
        nt = sb("nt", [P, 2, 12])
        nr = sb("nr", [P, 2, 12])
        rs = sb("rs", [P, 2, TG])
        nm = sb("nm", [P, 2, TG])
        mk = sb("mk", [P, 2, TG])
        qnb = sb("qnb", [P, 16])
        qnl = sb("qnl", [P, 16])
        qny = sb("qny", [P, 16])
        qnt = sb("qnt", [P, 2, 16])
        qnr = sb("qnr", [P, 16])

        w2t = sb("w2t", [P, 3, P])
        g2 = sb("g2", [P, 2, P])
        zT2 = sb("zT2", [P, B, P])
        uT = sb("uT", [P, B, P])
        att = sb("att", [P, B, P])
        v2 = sb("v2", [P, B, P])
        den = sb("den", [P, B, H])
        xl3 = sb("xl3", [P, B, P])
        zT3 = sb("zT3", [P, B, P])
        logit = sb("logit", [P, B, E])
        top = sb("top", [P, B, 8])
        topi = sb("topi", [P, B, 8], U32)
        topf = sb("topf", [P, B, 2])
        dif = sb("dif", [P, B])
        ex = sb("ex", [P, B])
        wt2 = sb("wt2", [P, B, 2])
        ex1 = sb("ex1", [P, B])
        we0 = sb("we0", [P, B, E])
        we = sb("we", [P, B, E])
        acc = sb("acc", [P, B, 2, P])

        pT = ps("pT", [P, TG, P])
        pK = [ps(f"pK{i}", [P, TG * P]) for i in range(2)]
        pS = [ps(f"pS{i}", [P, TG * H, P]) for i in range(2)]
        pY = ps("pY", [P, 512])
        SA, SB_ = pS[0][:, 0:4, :], pS[0][:, 4:8, :]
        SC, SD = pS[1][:, 0:4, :], pS[1][:, 4:8, :]

        s_x = sem("s_x_loaded")
        s_w1 = sem("s_first_weights_loaded")
        s_bc = sem("s_vectors_loaded")
        s_w2 = sem("s_later_weights_loaded")
        s_mask = sem("s_mask_loaded")
        s_exp_w = sem("s_expert_weights_loaded")
        s_ctx = [sem(f"s_context_loaded{i}") for i in range(GPB)]
        s_out = sem("s_out_stored")

        dv = sem("s_vector_step")
        s_maskf = sem("s_mask_float")
        s_amat = sem("s_a_ready")
        s_lnin = sem("s_latent_variance")
        s_lnout = sem("s_latent_rsqrt")
        s_zl = sem("s_latents_normalised")
        s_pe0 = sem("s_weight_products")
        s_wcopy = sem("s_weight_products_copied")
        s_lT = sem("s_latents_transposed")
        s_lTc = sem("s_latents_transposed_copied")
        s_qk = sem("s_q_and_k_of_latents")
        s_qksq = sem("s_q_and_k_squared")
        s_qnb = sem("s_q_and_k_sums")
        s_qny = sem("s_q_and_k_rsqrt")
        s_qg = sem("s_q_scaled")
        s_qT = sem("s_q_transposed")
        s_qTc = sem("s_q_transposed_copied")
        s_qw = sem("s_qw_product")
        s_qwc = sem("s_qw_copied")
        s_siml = sem("s_latent_scores")
        s_simlc = sem("s_latent_scores_scaled")
        s_probl = sem("s_latent_probs")
        s_yl = sem("s_latent_sums")
        s_ylc = sem("s_latent_sums_copied")

        s_lns = sem("s_group_scale_ready")
        s_z = sem("s_group_normalised")
        s_slot = sem("s_slot_free_for_pool")
        s_T = sem("s_group_transposed")
        s_Tc = sem("s_group_transposed_copied")
        s_K = sem("s_group_keys")
        s_Ksq = sem("s_group_keys_squared")
        s_nb = sem("s_group_sums_ready")
        s_ny = sem("s_group_rsqrt")
        s_S = sem("s_group_scores")
        s_Sc = sem("s_group_scores_scaled")
        s_P = sem("s_group_probs")
        s_PV = sem("s_group_summed")
        s_Y = sem("s_batch_sums_copied")

        s_t = {n: sem("s_tail_" + n) for n in
               ("o", "var1", "rsq1", "z2", "T2", "T2c", "u", "uc", "sv", "att", "v2", "y2", "var2", "rsq2",
                "z3", "T3", "T3c", "logit", "dif", "exp", "e", "acc")}

        block = ctx.enter_context(nc.Block())

        def has(b, i, k):
            return not isinstance(b, int) or 0 <= GPB * b + i + k < NG

        def run_steps(eng, step):
            for i in range(GPB):
                step(-1, i)
            with eng.Fori(0, B - 1) as b:
                for i in range(GPB):
                    step(b, i)
            for i in range(GPB):
                step(B - 1, i)

        @block.sync
        def _(sp):
            sp.dma_start(xin[:], x.rearrange("b s d -> s b d")).then_inc(s_x, 16)
            sp.dma_start(w1[:], first).then_inc(s_w1, 16)
            src = ctx_x.rearrange("b (p j t) d -> j p b (t d)", p=P, j=GPB)

            def load(b, i):
                if isinstance(b, int) and b < 0:
                    pass
                else:
                    sp.wait_ge(s_z, (TG + 1) * (GPB * b + i + 1))
                sp.dma_start(xctx[:, i, :, :].rearrange("p t d -> p (t d)"),
                             src[i, :, bass.ds(b + 1, 1), :].rearrange("p b n -> p (b n)")).then_inc(s_ctx[i], 16)

            for i in range(GPB):
                load(-1, i)
            sp.dma_start(w2[:], later).then_inc(s_w2, 16)
            with sp.Fori(0, B - 1) as b:
                for i in range(GPB):
                    load(b, i)
            sp.dma_start(wexp[:], experts.rearrange("e d h -> d e h")).then_inc(s_exp_w, 16)
            sp.wait_ge(s_t["acc"], B)
            sp.dma_start(out.rearrange("b s d -> s b d"), xmid[:]).then_inc(s_out, 16)
            sp.wait_ge(s_out, 16)

        @block.gpsimd
        def _(pool):
            pool.dma_start(mask8[:], mask.rearrange("b (p t) -> p b t", p=P)).then_inc(s_mask, 16)

            def step(b, i):
                if has(b, i, 4):
                    g4 = GPB * b + i + 4
                    pool.wait_ge(s_mask, 16)
                    pool.wait_ge(s_lns, g4 + 1)
                    if not (isinstance(b, int) and b < 0):
                        pool.wait_ge(s_PV, g4 + 1)
                    pool.sem_inc(s_slot, 1)
                    for t in range(TG):
                        nc.gpsimd.tensor_scalar(zt[:, i, t, 0:P - 1], xctx[:, i, t, 0:P - 1], rs[:, i % 2, t:t + 1],
                                                nm[:, i % 2, t:t + 1], ALU.mult, ALU.add).then_inc(s_z, 1)
                    nc.gpsimd.tensor_copy(zt[:, i, :, P - 1], mk[:, i % 2, :]).then_inc(s_z, 1)

            run_steps(pool, step)

        @block.scalar
        def _(act):
            act.preload_act_table_set("natural_log_exp_and_others")
            act.dma_start(bc[:], bcast.partition_broadcast(P)).then_inc(s_bc, 16)
            act.dma_start(row[:], rows).then_inc(s_bc, 16)

            def rsqrt_guess(src, mid, dst, ready, done, n):
                act.wait_ge(ready, n)
                nc.scalar.activation(mid, src, ACT.Ln).then_inc(done, 1)
                act.wait_ge(done, 2 * n - 1)
                nc.scalar.activation(dst, mid, ACT.Exp, scale=-0.5).then_inc(done, 1)

            def copy(dst, src, ready, n, done):
                act.wait_ge(ready, n)
                nc.scalar.copy(dst, src).then_inc(done, 1)

            rsqrt_guess(qnb[:, 0:B], qnl[:, 0:B], qny[:, 0:B], s_lnin, s_lnout, 1)
            rsqrt_guess(qnb[:, 4:4 + B], qnl[:, 4:4 + B], qny[:, 4:4 + B], s_lnin, s_lnout, 2)
            copy(wproj[:], SA[:, 0:3, :], s_pe0, 1, s_wcopy)
            copy(wT[:].rearrange("p a b d -> p (a b) d"), SB_, s_pe0, 2, s_wcopy)
            copy(zlT[:], pT[:], s_lT, 1, s_lTc)
            for n in range(2):
                act.wait_ge(s_qk, n + 1)
                nc.scalar.activation(qksq[:, n, :], pK[n][:], ACT.Square).then_inc(s_qksq, 1)
            for h in range(H):
                copy(vo[:, :, h, 0:P], [SC, SD][h][:, 0:2, :], s_pe0, 3, s_wcopy)
            rsqrt_guess(qnb[:], qnl[:], qny[:], s_qnb, s_qny, 1)
            copy(qT[:], pT[:], s_qT, 1, s_qTc)
            for n in range(2 * H):
                copy(qw[:, n // H, :, n % H, :], [SA, SB_, SC, SD][n], s_qw, n + 1, s_qwc)
            copy(w2t[:], pK[0][:, 0:3 * P].rearrange("p (a d) -> p a d", a=3), s_pe0, 4, s_wcopy)
            copy(g2[:], pK[1][:, 0:2 * P].rearrange("p (a d) -> p a d", a=2), s_pe0, 5, s_wcopy)
            act.wait_ge(s_simlc, 1)
            nc.scalar.activation(probl[:].rearrange("p b n -> p (b n)"), siml[:].rearrange("p a n -> p (a n)"),
                                 ACT.Exp).then_inc(s_probl, 1)
            copy(y[:, 0].rearrange("p b h n -> p (b h) n"), pS[1][:], s_yl, 1, s_ylc)

            def step(b, i):
                g = GPB * b + i
                if has(b, i, 2):
                    act.wait_ge(s_K, g + 3)
                    if not (isinstance(b, int) and g + 2 < 1):
                        act.wait_ge(s_nb, g + 4)
                    nc.scalar.activation(ksq[:], pK[i % 2][:], ACT.Square).then_inc(s_Ksq, 1)
                if has(b, i, 1):
                    k = (i + 1) % GPB
                    act.wait_ge(s_Sc, g + 2)
                    act.wait_ge(s_PV, g + 2)
                    nc.scalar.activation(prob[:, k].rearrange("p t n -> p (t n)"),
                                         sims[:, k % 2].rearrange("p a n -> p (a n)"), ACT.Exp).then_inc(s_P, 1)
                if has(b, i, 2) or has(b, i, 4):
                    lo, hi = (0 if has(b, i, 2) else 8), (12 if has(b, i, 4) else 8)
                    n = g + 5
                    act.wait_ge(s_nb, n)
                    nc.scalar.activation(nl[:, lo:hi], nb[:, lo:hi], ACT.Ln).then_inc(s_ny, 1)
                    act.wait_ge(s_ny, 2 * n - 1)
                    nc.scalar.activation(ny[:, lo:hi], nl[:, lo:hi], ACT.Exp, scale=-0.5).then_inc(s_ny, 1)
                if has(b, i, 0) and i == GPB - 1:
                    act.wait_ge(s_PV, GPB + g + 1)
                    nc.scalar.copy(y[:, 1].rearrange("p b h n -> p b (h n)")[:, bass.ds(b, 1), :]
                                   .rearrange("p o n -> p (o n)"), pY[:, 0:H * P]).then_inc(s_Y, 1)
                if has(b, i, 3):
                    act.wait_ge(s_T, g + 4)
                    nc.scalar.copy(zT[:, (i + 1) % 2], pT[:]).then_inc(s_Tc, 1)

            run_steps(act, step)

            rsqrt_guess(qnb[:, 0:B], qnl[:, 0:B], qny[:, 0:B], s_t["var1"], s_t["rsq1"], 1)
            copy(zT2[:], pT[:], s_t["T2"], 1, s_t["T2c"])
            copy(uT[:].rearrange("p b s -> p (b s)"), pK[0][:], s_t["u"], 1, s_t["uc"])
            copy(v2[:].rearrange("p b s -> p (b s)"), pK[1][:], s_t["sv"], 2, s_t["v2"])
            rsqrt_guess(qnb[:, 0:B], qnl[:, 0:B], qny[:, 0:B], s_t["var2"], s_t["rsq2"], 1)
            copy(zT3[:], pT[:], s_t["T3"], 1, s_t["T3c"])
            act.wait_ge(s_t["dif"], 1)
            nc.scalar.activation(ex[:], dif[:], ACT.Exp).then_inc(s_t["exp"], 1)

        @block.tensor
        def _(pe):
            mm = nc.tensor.matmul

            pe.sem_inc(s_PV, GPB)
            pe.sem_inc(s_Y, 1)
            pe.wait_ge(s_amat, 2)
            pe.wait_ge(s_w1, 16)
            mm(SA[:, 0, :], amat[:, 0, :], w1_["wq"])
            mm(SA[:, 1, :], amat[:, 0, :], w1_["wk"])
            mm(SA[:, 2, :], amat[:, 1, :], w1_["wk"]).then_inc(s_pe0, 1)
            am = amat[:].rearrange("p a d -> p (a d)")
            mm(SB_[:, 0:2, :].rearrange("p a d -> p (a d)"), w1_["wk"], am)
            mm(SB_[:, 2:4, :].rearrange("p a d -> p (a d)"), w1_["wv"], am).then_inc(s_pe0, 1)
            pe.wait_ge(s_zl, 2)
            for b in range(B):
                last = nc.tensor.transpose(pT[:, b, :], zl[:, b, :], ident)
            last.then_inc(s_lT, 1)
            pe.wait_ge(s_wcopy, 1)
            pe.wait_ge(s_lTc, 1)
            for n in range(2):
                for b in range(B):
                    last = mm(pK[n][:, b * P:(b + 1) * P], zlT[:, b, :], wproj[:, n, :])
                last.then_inc(s_qk, 1)
            pe.wait_ge(s_wcopy, 2)
            for a in range(2):
                for h in range(H):
                    r = slice(h * DH, (h + 1) * DH)
                    last = mm([SC, SD][h][:, a, :], wT[r, 1, a, :], w1_["wout"][r, :])
            last.then_inc(s_pe0, 1)
            pe.wait_ge(s_qg, 1)
            for b in range(B):
                last = nc.tensor.transpose(pT[:, b, :], qg[:, b, :], ident)
            last.then_inc(s_qT, 1)
            pe.wait_ge(s_qTc, 1)
            pe.wait_ge(s_wcopy, 4)
            for n in range(2 * H):
                a, h = n // H, n % H
                r = slice(h * DH, (h + 1) * DH)
                mm([SA, SB_, SC, SD][n].rearrange("p b d -> p (b d)"), wT[r, 0, a, :],
                   qT[r, :, :].rearrange("p b d -> p (b d)")).then_inc(s_qw, 1)
            pe.wait_ge(s_w2, 16)
            pe.wait_ge(s_bc, 32)
            pe.wait_ge(s_qg, 1)
            pe.wait_ge(s_qksq, 2)
            for n, (w, o) in enumerate((("wkT", "bk"), ("wvT", "bv"), ("wqT", "bq"))):
                mm(pK[0][:, n * P:(n + 1) * P], w2_[w], w1_["cent"], start=True, stop=False)
                last = mm(pK[0][:, n * P:(n + 1) * P], row_[o], row_["e_last"], start=False, stop=True)
            last.then_inc(s_pe0, 1)
            pe.wait_ge(s_wcopy, 5)
            mm(pK[1][:, 0:P], w2t[:, 2, :], w2t[:, 0, :])
            mm(pK[1][:, P:2 * P], w2t[:, 1, :], w2_["woT"]).then_inc(s_pe0, 1)
            pe.wait_ge(s_qwc, 4)
            for b in range(B):
                last = mm(pS[0][:, 2 * b:2 * b + 2, :].rearrange("p h n -> p (h n)"), zlT[:, b, :],
                          qw[:, 0, b].rearrange("p h n -> p (h n)"))
            last.then_inc(s_siml, 1)
            pe.wait_ge(s_probl, 1)
            for b in range(B):
                last = mm(pS[1][:, 2 * b:2 * b + 2, :].rearrange("p h n -> p (h n)"), zl[:, b, :], probl[:, b, :])
            last.then_inc(s_yl, 1)
            pe.wait_ge(s_ylc, 1)
            pe.wait_ge(s_wcopy, 6)

            def step(b, i):
                g = GPB * b + i
                if has(b, i, 0):
                    pe.wait_ge(s_P, g + 1)
                    if i == 0:
                        pe.wait_ge(s_Y, b + 1)
                    for t in range(TG):
                        last = mm(pY[:, 0:H * P], zt[:, i, t, :], prob[:, i, t, :],
                                  start=(i == 0 and t == 0), stop=(i == GPB - 1 and t == TG - 1))
                    last.then_inc(s_PV, 1)
                if has(b, i, 2):
                    k = i % 2
                    pe.wait_ge(s_Tc, g + 3)
                    if not (isinstance(b, int) and g + 2 < 2):
                        pe.wait_ge(s_Ksq, g + 1)
                    for t in range(TG):
                        last = mm(pK[k][:, t * P:(t + 1) * P], zT[:, k, t, :], wproj[:, 2, :])
                    last.then_inc(s_K, 1)
                    if not (isinstance(b, int) and g + 2 < 2):
                        pe.wait_ge(s_Sc, g + 1)
                    q = qw[:, 1].rearrange("p b h n -> p b (h n)")[:, bass.ds(b + (i + 2) // GPB, 1), :]\
                        .rearrange("p o n -> p (o n)")
                    for t in range(TG):
                        last = mm(pS[k][:, 2 * t:2 * t + 2, :].rearrange("p h n -> p (h n)"), zT[:, k, t, :], q)
                    last.then_inc(s_S, 1)
                if has(b, i, 3):
                    pe.wait_ge(s_z, (TG + 1) * (g + 4))
                    if not (isinstance(b, int) and g + 3 < 1):
                        pe.wait_ge(s_Tc, g + 3)
                    for t in range(TG):
                        last = nc.tensor.transpose(pT[:, t, :], zt[:, (i + 3) % GPB, t, :], ident)
                    last.then_inc(s_T, 1)

            run_steps(pe, step)

            bank = [pK[0][:, :], pK[1][:, :], SA.rearrange("p a n -> p (a n)"), SB_.rearrange("p a n -> p (a n)")]
            pe.wait_ge(s_Y, B + 1)
            pe.wait_ge(s_Ksq, NG)
            pe.wait_ge(s_Sc, NG)
            for b in range(B):
                for h in range(H):
                    o = bank[b][:, h * (P + 1):(h + 1) * (P + 1)]
                    mm(o, y[:, 0, b, h, :], vo[:, 0, h, :], start=True, stop=False)
                    last = mm(o, y[:, 1, b, h, :], vo[:, 1, h, :], start=False, stop=True)
                last.then_inc(s_t["o"], 1)
            pe.wait_ge(s_t["z2"], 2)
            for b in range(B):
                last = nc.tensor.transpose(pT[:, b, :], zl[:, b, :], ident)
            last.then_inc(s_t["T2"], 1)
            pe.wait_ge(s_t["T2c"], 1)
            mm(pK[0][:], g2[:, 0, :], zT2[:].rearrange("p b s -> p (b s)")).then_inc(s_t["u"], 1)
            pe.wait_ge(s_t["uc"], 1)
            for b in range(B):
                last = mm(pS[0][:, b, :], zT2[:, b, :], uT[:, b, :])
            last.then_inc(s_t["sv"], 1)
            for b in range(B):
                last = mm(pK[1][:, b * P:(b + 1) * P], zT2[:, b, :], g2[:, 1, :])
            last.then_inc(s_t["sv"], 1)
            pe.wait_ge(s_t["att"], 1)
            pe.wait_ge(s_t["v2"], 1)
            for b in range(B):
                last = mm(pS[1][:, b, :], att[:, b, :], v2[:, b, :])
            last.then_inc(s_t["y2"], 1)
            pe.wait_ge(s_t["z3"], 1)
            for b in range(B):
                last = nc.tensor.transpose(pT[:, b, :], xl3[:, b, :], ident)
            last.then_inc(s_t["T3"], 1)
            pe.wait_ge(s_t["T3c"], 1)
            for b in range(B):
                last = mm(pY[:, b * E:(b + 1) * E], zT3[:, b, :], w2_["gate"])
            last.then_inc(s_t["logit"], 1)
            pe.wait_ge(s_exp_w, 16)
            for b in range(B):
                if b >= 2:
                    pe.wait_ge(s_t["acc"], b - 1)
                for k in range(2):
                    last = mm(pS[b % 2][:, 4 * k:4 * k + 4, :].rearrange("p e h -> p (e h)"), zT3[:, b, :],
                              wexp[:, 4 * k:4 * k + 4, :].rearrange("p e h -> p (e h)"))
                last.then_inc(s_t["e"], 1)

        @block.vector
        def _(dve):
            v = nc.vector
            chain = [0]

            def link(ins):
                chain[0] += 1
                ins.then_inc(dv, 1)
                dve.wait_ge(dv, chain[0])

            def ln_terms(src, tmp, var, ln):
                for t in range(TG):
                    last = v.bn_stats(bst[:, t, :], src[:, t, :])
                ln(last)
                v.tensor_tensor(tmp[:, 0], bst[:, :, 1], bst[:, :, 4], ALU.add)
                ln(v.tensor_tensor(tmp[:, 1], bst[:, :, 1], bst[:, :, 4], ALU.subtract))
                v.scalar_tensor_tensor(tmp[:, 2], bst[:, :, 2], LN_EPS * P, bst[:, :, 5], ALU.add, ALU.add)
                ln(v.scalar_tensor_tensor(tmp[:, 3], tmp[:, 1], 0.25, tmp[:, 1], ALU.mult, ALU.mult))
                return v.scalar_tensor_tensor(var, tmp[:, 2], 1.0 / P, tmp[:, 3], ALU.mult, ALU.add)

            def newton(val, guess, tmp, dst, ln):
                ln(v.tensor_tensor(tmp[:, 0], guess, guess, ALU.mult))
                ln(v.scalar_tensor_tensor(tmp[:, 1], tmp[:, 0], -0.5, val, ALU.mult, ALU.mult))
                return v.scalar_tensor_tensor(dst, tmp[:, 1], 1.5, guess, ALU.add, ALU.mult)

            dve.wait_ge(s_w1, 16)
            for a, n in enumerate("lx"):
                link(v.tensor_scalar(amat[:, a, :], w1_["cent"], w1_["g_" + n], None, ALU.mult))
                v.tensor_copy(amat[:, a, P - 1:P], w1_["b_" + n]).then_inc(s_amat, 1)
                v.tensor_copy(vo[:, a, :, P], ident[:, P - 1:P].to_broadcast([P, H]))

            dve.wait_ge(s_x, 16)
            ln_terms(xin, stt[:, 0:4], qnb[:, 0:B], link).then_inc(s_lnin, 1)
            dve.wait_ge(s_lnin, 1)
            dve.wait_ge(s_lnout, 2)
            link(newton(qnb[:, 0:B], qny[:, 0:B], qnt[:, :, 0:B], qnr[:, 0:B], link))
            link(v.tensor_tensor(stt[:, 4], qnr[:, 0:B], qnr[:, 0:B], ALU.mult))
            v.tensor_scalar(qnb[:, 4:4 + B], stt[:, 4], -LN_EPS, 1.0 + LN_EPS, ALU.mult, ALU.add).then_inc(s_lnin, 1)
            dve.wait_ge(s_lnout, 4)
            dve.wait_ge(s_lnin, 2)
            link(newton(qnb[:, 4:4 + B], qny[:, 4:4 + B], qnt[:, :, 4:4 + B], qnr[:, 4:4 + B], link))
            link(v.tensor_tensor(stt[:, 5], qnr[:, 0:B], qnr[:, 4:4 + B], ALU.mult))
            link(v.scalar_tensor_tensor(stt[:, 4], stt[:, 0], -0.5, stt[:, 5], ALU.mult, ALU.mult))

            def normalise(dst, src, scale, offset, done):
                for b in range(B):
                    last = v.tensor_scalar(dst[:, b, :], src[:, b, :], scale[:, b:b + 1], offset[:, b:b + 1],
                                           ALU.mult, ALU.add)
                last.then_inc(done, 1)

            normalise(zl, xin, stt[:, 5], stt[:, 4], s_zl)
            dve.wait_ge(s_zl, 1)
            v.memset(zl[:, :, P - 1], 1.0).then_inc(s_zl, 1)
            dve.wait_ge(s_bc, 32)
            v.tensor_tensor(xres[:], xin[:], bc_["b_out"].rearrange("p (o d) -> p o d", o=1).to_broadcast([P, B, P]), ALU.add)
            link(v.scalar_tensor_tensor(gam[:], bc_["q_gamma"].rearrange("p (o d) -> p o d", o=1).to_broadcast([P, H, DH]),
                                   float(DH) ** 0.5,
                                   bc_["k_gamma"].rearrange("p (o d) -> p o d", o=1).to_broadcast([P, H, DH]),
                                   ALU.mult, ALU.mult))
            dve.wait_ge(s_mask, 16)
            v.tensor_copy(maskf[:], mask8[:]).then_inc(s_maskf, 1)
            dve.wait_ge(s_maskf, 1)

            dve.wait_ge(s_qksq, 2)
            link(v.tensor_reduce(qnb[:], qksq[:].rearrange("p a (n d) -> p (a n) d", d=DH), AX.X, ALU.add))
            v.tensor_scalar(qnb[:], qnb[:], SSQ_MIN, None, ALU.max).then_inc(s_qnb, 1)
            dve.wait_ge(s_qnb, 1)
            dve.wait_ge(s_qny, 2)
            link(newton(qnb[:], qny[:], qnt[:], qnr[:], link))
            link(v.tensor_tensor(qn[:], pK[0][:].rearrange("p (n d) -> p n d", d=DH),
                                 qnr[:, 0:8].rearrange("p (n o) -> p n o", o=1).to_broadcast([P, B * H, DH]), ALU.mult))
            v.tensor_tensor(qg[:], qn[:].rearrange("p (b h) d -> p b (h d)", b=B),
                            gam[:].rearrange("p (o h) d -> p o (h d)", o=1).to_broadcast([P, B, P]), ALU.mult)\
                .then_inc(s_qg, 1)
            dve.wait_ge(s_siml, 1)
            v.tensor_tensor(siml[:], pS[0][:],
                            qnr[:, 8:16].rearrange("p (n o) -> p n o", o=1).to_broadcast([P, B * H, P]), ALU.mult)\
                .then_inc(s_simlc, 1)

            base = chain[0]
            links = [0]
            LINKS = 10

            def step(b, i):
                g = GPB * b + i
                n = [0]

                def ln(ins):
                    n[0] += 1
                    ins.then_inc(dv, 1)
                    dve.wait_ge(dv, base + LINKS * (g + 4) + n[0])

                lns, keys = has(b, i, 4), has(b, i, 2)
                first_step = isinstance(b, int) and g == -4
                if lns:
                    dve.wait_ge(s_ctx[i], 16 * (b + 2))
                    if not first_step:
                        dve.wait_ge(s_ny, 2 * (g + 4))
                    last = ln_terms(xctx[:, i], stt[:, 0:4], nb[:, 8:12], ln)
                    if not keys:
                        last.then_inc(s_nb, 1)
                    else:
                        ln(last)
                if keys:
                    dve.wait_ge(s_Ksq, g + 3)
                    ln(v.tensor_reduce(nb[:, 0:8], ksq[:].rearrange("p (n d) -> p n d", d=DH), AX.X, ALU.add))
                    v.tensor_scalar(nb[:, 0:8], nb[:, 0:8], SSQ_MIN, None, ALU.max).then_inc(s_nb, 1)
                if lns or keys:
                    lo, hi = (0 if keys else 8), (12 if lns else 8)
                    dve.wait_ge(s_ny, 2 * (g + 5))
                    dve.wait_ge(s_nb, g + 5)
                    ln(newton(nb[:, lo:hi], ny[:, lo:hi], nt[:, :, lo:hi], nr[:, i % 2, lo:hi], ln))
                if lns:
                    if not (isinstance(b, int) and g + 4 < 2):
                        dve.wait_ge(s_z, (TG + 1) * (g + 3))
                    mg = maskf[:, bass.ds(b + 1, 1), i * TG:(i + 1) * TG].rearrange("p o t -> p (o t)")
                    v.tensor_copy(mk[:, i % 2, :], mg)
                    ln(v.tensor_tensor(rs[:, i % 2, :], nr[:, i % 2, 8:12], mg, ALU.mult))
                    v.scalar_tensor_tensor(nm[:, i % 2, :], stt[:, 0], -0.5, rs[:, i % 2, :], ALU.mult, ALU.mult)\
                        .then_inc(s_lns, 1)
                if keys:
                    dve.wait_ge(s_S, g + 3)
                    if not (isinstance(b, int) and g + 2 < 2):
                        dve.wait_ge(s_P, g + 1)
                    v.tensor_tensor(sims[:, i % 2], pS[i % 2][:],
                                    nr[:, i % 2, 0:8].rearrange("p (n o) -> p n o", o=1).to_broadcast([P, TG * H, P]),
                                    ALU.mult).then_inc(s_Sc, 1)
                assert n[0] <= LINKS
                dve.sem_inc(dv, LINKS - n[0])

            run_steps(dve, step)
            chain[0] = base + LINKS * (NG + 4)

            bank = [pK[0][:, :], pK[1][:, :], SA.rearrange("p a n -> p (a n)"), SB_.rearrange("p a n -> p (a n)")]
            for b in range(B):
                dve.wait_ge(s_t["o"], b + 1)
                o = bank[b][:, 0:H * (P + 1)].rearrange("p (h n) -> p h n", h=H)
                link(v.reciprocal(den[:, b, :], o[:, :, P]))
                link(v.scalar_tensor_tensor(xmid[:, b, :], o[:, 0, 0:P], den[:, b, 0:1], xres[:, b, :], ALU.mult, ALU.add))
                link(v.scalar_tensor_tensor(xres[:, b, :], o[:, 1, 0:P], den[:, b, 1:2], xmid[:, b, :], ALU.mult, ALU.add))

            def layer_norm(src, dst, var_sem, rsq_sem, done):
                ln_terms(src, stt[:, 0:4], qnb[:, 0:B], link).then_inc(var_sem, 1)
                dve.wait_ge(var_sem, 1)
                dve.wait_ge(rsq_sem, 2)
                link(newton(qnb[:, 0:B], qny[:, 0:B], qnt[:, :, 0:B], qnr[:, 0:B], link))
                link(v.scalar_tensor_tensor(stt[:, 4], stt[:, 0], -0.5, qnr[:, 0:B], ALU.mult, ALU.mult))
                normalise(dst, src, qnr, stt[:, 4], done)

            layer_norm(xres, zl, s_t["var1"], s_t["rsq1"], s_t["z2"])
            dve.wait_ge(s_t["z2"], 1)
            v.memset(zl[:, :, P - 1], 1.0).then_inc(s_t["z2"], 1)
            link(v.tensor_tensor(xmid[:], xres[:], bc_["b_o"].rearrange("p (o d) -> p o d", o=1).to_broadcast([P, B, P]), ALU.add))
            dve.wait_ge(s_t["sv"], 1)
            v.tensor_tensor(att[:], pS[0][:, 0:B, :],
                            w2_["decay"].rearrange("p (o d) -> p o d", o=1).to_broadcast([P, B, P]), ALU.mult)\
                .then_inc(s_t["att"], 1)
            dve.wait_ge(s_t["y2"], 1)
            link(v.tensor_tensor(xres[:], xmid[:], pS[1][:, 0:B, :], ALU.add))
            layer_norm(xres, xl3, s_t["var2"], s_t["rsq2"], s_t["z3"])
            dve.wait_ge(s_t["logit"], 1)
            link(v.tensor_copy(logit[:], pY[:, 0:B * E].rearrange("p (b e) -> p b e", b=B)))
            for b in range(B):
                last = v.max(top[:, b, :], logit[:, b, :])
            link(last)
            for b in range(B):
                last = v.max_index(topi[:, b, :], top[:, b, :], logit[:, b, :])
            link(last)
            v.tensor_tensor(dif[:], top[:, :, 1], top[:, :, 0], ALU.subtract).then_inc(s_t["dif"], 1)
            link(v.tensor_copy(topf[:], topi[:, :, 0:2]))
            dve.wait_ge(s_t["exp"], 1)
            link(v.tensor_scalar(ex1[:], ex[:], 1.0, None, ALU.add))
            link(v.reciprocal(wt2[:, :, 0], ex1[:]))
            link(v.tensor_tensor(wt2[:, :, 1], ex[:], wt2[:, :, 0], ALU.mult))
            for b in range(B):
                v.tensor_scalar(we0[:, b, :], bc_["iota"], topf[:, b, 0:1], wt2[:, b, 0:1], ALU.is_equal, ALU.mult)
                last = v.tensor_scalar(we[:, b, :], bc_["iota"], topf[:, b, 1:2], wt2[:, b, 1:2], ALU.is_equal, ALU.mult)
            link(last)
            link(v.tensor_tensor(we[:], we[:], we0[:], ALU.add))
            for b in range(B):
                dve.wait_ge(s_t["e"], b + 1)
                src = xres[:, b, :]
                for e in range(E):
                    dst = xmid[:, b, :] if e == E - 1 else acc[:, b, e % 2, :]
                    last = v.scalar_tensor_tensor(dst, pS[b % 2][:, e, :], we[:, b, e:e + 1], src, ALU.mult, ALU.add)
                    if e < E - 1:
                        link(last)
                    src = dst
                last.then_inc(s_t["acc"], 1)


def kernel(**inputs):
    import concourse.bacc as bacc
    from concourse.bass_utils import run_bass_kernel_spmd as run

    a = {k.replace("L0_", ""): np.ascontiguousarray(v) for k, v in inputs.items()}
    eye = np.eye(P, dtype=np.float32)
    cent = eye.copy()
    cent[P - 1, :] = -1.0
    cent[:, P - 1] = 0.0
    t = np.arange(P)
    lag = t[None, :] - 1 - t[:, None]
    decay = np.where(lag >= 0, LR * DECAY ** np.maximum(lag, 0).astype(np.float64), 0.0).astype(np.float32)
    e_last = eye[P - 1]
    wkv = a["xattn_W_kv"]
    first = np.concatenate([a["xattn_ln_l_g"][:, None], a["xattn_ln_l_b"][:, None], a["xattn_ln_x_g"][:, None],
                            a["xattn_ln_x_b"][:, None], eye, cent, a["xattn_W_q"], wkv, a["xattn_W_out"]], axis=1)
    later = np.concatenate([decay, a["attn_Wk"].T, a["attn_Wv"].T, a["attn_Wq"].T, a["attn_Wo"].T,
                            a["ffn_gate_w"].T], axis=1)
    rows = np.concatenate([a["attn_bk"], a["attn_bv"], a["attn_bq"], e_last])[None]
    bcast = np.concatenate([a["xattn_b_out"], a["attn_bo"], a["xattn_q_gamma"], a["xattn_k_gamma"],
                            np.arange(E, dtype=np.float32)])
    arrays = {"x": a["x"], "ctx": a["ctx_1024"], "mask": a["mask_BxS2_bk0"], "first": first,
              "later": later, "rows": rows, "bcast": bcast, "experts": a["ffn_weight"]}
    arrays = {k: np.ascontiguousarray(v) for k, v in arrays.items()}
    nc = bacc.Bacc("TRN2", target_bir_lowering=False, num_devices=1)
    args = [nc.dram_tensor(k, v.shape, mybir.dt.from_np(v.dtype), kind="ExternalInput").ap() for k, v in arrays.items()]
    out = nc.dram_tensor("out", (B, P, P), F32, kind="ExternalOutput").ap()
    build(nc, *args, out)
    return run(nc, [arrays], core_ids=[0]).results[0]["out"]
```

```python
from contextlib import ExitStack

import concourse.bass as bass
import numpy as np
from concourse import mybir

ALU = mybir.AluOpType
ACT = mybir.ActivationFunctionType
F32 = mybir.dt.float32
U8 = mybir.dt.uint8
U32 = mybir.dt.uint32
AX = mybir.AxisListType

P = 128
B = 4
S2 = 2048
H = 2
DH = P // H
E = 8
TG = 4
TPB = S2 // P
GPB = TPB // TG
NG = B * GPB
LN_EPS = 1e-5
SSQ_MIN = DH * 1e-16
DECAY, LR = 0.99, 0.01
WARM = 2

FIRST = dict(g_l=(0, 1), b_l=(1, 2), g_x=(2, 3), b_x=(3, 4), g_q=(4, 5), g_k=(5, 6), ident=(6, 134), cent=(134, 262),
             wq=(262, 390), wk=(390, 518))
SECOND = dict(wv=(0, 128), wout=(128, 256))
LATER = dict(decay=(0, 128), wkT=(128, 256), wvT=(256, 384), wqT=(384, 512), woT=(512, 640), gate=(640, 648))
ROWS = dict(bk=(0, 128), bv=(128, 256), bq=(256, 384), e_last=(384, 512))
BCAST = dict(b_out=(0, 128), b_o=(128, 256), q_gamma=(256, 320), k_gamma=(320, 384), iota=(384, 392))
SIM_MAX = 80.0


def build(nc, x, ctx_x, mask, first, second, later, rows, bcast, experts, out):
    ctx = ExitStack()
    with ctx:
        def sb(name, shape, dt=F32):
            return ctx.enter_context(nc.sbuf_tensor(name, shape, dt))

        def ps(name, shape):
            return ctx.enter_context(nc.psum_tensor(name, shape, F32))

        def sem(name):
            return ctx.enter_context(nc.semaphore(name))

        w1 = sb("w1", [P, 518])
        w1b = sb("w1b", [P, 256])
        w2 = sb("w2", [P, 648])
        w1_ = {k: w1[:, a:z] for k, (a, z) in FIRST.items()}
        w1_.update({k: w1b[:, a:z] for k, (a, z) in SECOND.items()})
        w2_ = {k: w2[:, a:z] for k, (a, z) in LATER.items()}
        row = sb("row", [1, 512])
        row_ = {k: row[:, a:z] for k, (a, z) in ROWS.items()}
        bc = sb("bc", [P, 392])
        bc_ = {k: bc[:, a:z] for k, (a, z) in BCAST.items()}
        ident = w1_["ident"]
        wexp = sb("wexp", [P, E, P])
        mask8 = sb("mask8", [P, B, TPB], U8)
        maskf = sb("maskf", [P, B, TPB])

        xin = sb("xin", [P, B, P])
        xres = sb("xres", [P, B, P])
        xmid = sb("xmid", [P, B, P])
        xctx = sb("xctx", [P, GPB, TG, P])
        zt = sb("zt", [P, GPB, TG, P])
        zT = sb("zT", [P, 2, TG, P])
        ksq = sb("ksq", [P, TG * P])
        prob = sb("prob", [P, GPB, TG, H * P])

        amat = sb("amat", [P, 2, P])
        wproj = sb("wproj", [P, 3, P])
        wT = sb("wT", [P, 2, 2, P])
        vo = sb("vo", [P, 2, H, P + 1])
        gcol = sb("gcol", [P, 1])
        gprod = sb("gprod", [P, DH])
        gmax = sb("gmax", [P, 2])
        guard = sb("guard", [P, 1])
        warm = sb("warm", [P, 512])
        zl = sb("zl", [P, B, P])
        zlT = sb("zlT", [P, B, P])
        qksq = sb("qksq", [P, 2, B * P])
        qg = sb("qg", [P, B, P])
        qT = sb("qT", [P, B, P])
        qw = sb("qw", [P, 2, B, H, P])
        probl = sb("probl", [P, B, H * P])
        y = sb("y", [P, 2, B, H, P])

        bst = sb("bst", [P, TG, 6])
        stt = sb("stt", [P, 6, TG])
        nb = sb("nb", [P, 12])
        nl = sb("nl", [P, 12])
        ny = sb("ny", [P, 12])
        nt = sb("nt", [P, 2, 12])
        nr = sb("nr", [P, 2, 12])
        rs = sb("rs", [P, 2, TG])
        nm = sb("nm", [P, 2, TG])
        mk = sb("mk", [P, 2, TG])
        qnb = sb("qnb", [P, 16])
        qnl = sb("qnl", [P, 16])
        qny = sb("qny", [P, 16])
        qnt = sb("qnt", [P, 2, 16])
        qnr = sb("qnr", [P, 16])

        w2t = sb("w2t", [P, 3, P])
        g2 = sb("g2", [P, 2, P])
        zT2 = sb("zT2", [P, B, P])
        uT = sb("uT", [P, B, P])
        att = sb("att", [P, B, P])
        v2 = sb("v2", [P, B, P])
        den = sb("den", [P, B, H])
        xl3 = sb("xl3", [P, B, P])
        zT3 = sb("zT3", [P, B, P])
        mv = sb("mv", [P, B, 2])
        top = sb("top", [P, B, 8])
        topi = sb("topi", [P, B, 8], U32)
        topf = sb("topf", [P, B, 2])
        dif = sb("dif", [P, B])
        ex = sb("ex", [P, B])
        wt2 = sb("wt2", [P, B, 2])
        ex1 = sb("ex1", [P, B])
        hot = sb("hot", [P, B, 2, E])
        hotw = sb("hotw", [P, B, 2, E])
        we = sb("we", [P, B, E])
        wex = sb("wex", [P, 2, E, P])
        acc = sb("acc", [P, B, 2, P])

        pT = ps("pT", [P, TG, P])
        pK = [ps(f"pK{i}", [P, TG * P]) for i in range(2)]
        pS = [ps(f"pS{i}", [P, TG * H, P]) for i in range(2)]
        pY = ps("pY", [P, 512])
        SA, SB_ = pS[0][:, 0:4, :], pS[0][:, 4:8, :]
        SC, SD = pS[1][:, 0:4, :], pS[1][:, 4:8, :]

        s_x = sem("s_x_loaded")
        s_w1 = sem("s_first_weights_loaded")
        s_w1b = sem("s_value_weights_loaded")
        s_bc = sem("s_vectors_loaded")
        s_w2 = sem("s_later_weights_loaded")
        s_mask = sem("s_mask_loaded")
        s_exp_w = sem("s_expert_weights_loaded")
        s_ctx = [sem(f"s_context_loaded{i}") for i in range(GPB)]
        s_out = sem("s_out_stored")

        dv = sem("s_vector_step")
        s_maskf = sem("s_mask_float")
        s_amat = sem("s_a_ready")
        s_vo = sem("s_vo_last_column")
        s_lnin = sem("s_latent_variance")
        s_lnout = sem("s_latent_rsqrt")
        s_zl = sem("s_latents_normalised")
        s_pe0 = sem("s_weight_products")
        s_wcopy = sem("s_weight_products_copied")
        s_lT = sem("s_latents_transposed")
        s_lTc = sem("s_latents_transposed_copied")
        s_qk = sem("s_q_and_k_of_latents")
        s_qksq = sem("s_q_and_k_squared")
        s_qnb = sem("s_q_and_k_sums")
        s_qny = sem("s_q_and_k_rsqrt")
        s_qnr = sem("s_q_and_k_scales")
        s_qg = sem("s_q_scaled")
        s_qT = sem("s_q_transposed")
        s_qTc = sem("s_q_transposed_copied")
        s_qw = sem("s_qw_product")
        s_qwc = sem("s_qw_copied")
        s_siml = sem("s_latent_scores")
        s_warm = sem("s_zeros_ready")
        s_guard = sem("s_guard_ready")
        s_xres = sem("s_x_plus_b_out")
        s_probl = sem("s_latent_probs")
        s_yl = sem("s_latent_sums")
        s_ylc = sem("s_latent_sums_copied")

        s_lns = sem("s_group_scale_ready")
        s_z = sem("s_group_normalised")
        s_slot = sem("s_slot_free_for_pool")
        s_T = sem("s_group_transposed")
        s_Tc = sem("s_group_transposed_copied")
        s_K = sem("s_group_keys")
        s_Ksq = sem("s_group_keys_squared")
        s_nb = sem("s_group_sums_ready")
        s_ny = sem("s_group_rsqrt")
        s_S = sem("s_group_scores")
        s_nr = sem("s_group_key_scales")
        s_P = sem("s_group_probs")
        s_PV = sem("s_group_summed")
        s_Y = sem("s_batch_sums_copied")

        s_t = {n: sem("s_tail_" + n) for n in
               ("o", "res", "bo", "var1", "rsq1", "off1", "z2", "T2", "T2c", "u", "uc", "s", "v", "att", "v2", "y2",
                "var2", "rsq2", "off2", "z3", "T3", "T3c", "logit", "logc", "dif", "exp", "we", "e", "scaled",
                "sum", "acc")}

        PARTS = [(0, B - 1), (B - 1, B)]
        EXPERT_ORDER = [0, 2, 1, 3]
        o_banks = [pT[:].rearrange("p t d -> p (t d)"), pK[0][:, :], pK[1][:, :]]

        def o_at(b, h):
            if b < B - 1:
                return o_banks[b][:, h * (P + 1):(h + 1) * (P + 1)]
            return [SA, SB_][h].rearrange("p a n -> p (a n)")[:, 0:P + 1]

        K0, K1 = [p[:].rearrange("p (n d) -> p n d", d=P) for p in pK]
        PT, PY = pT[:], pY[:].rearrange("p (n d) -> p n d", d=P)
        t2_bank, u_bank, v_bank, s_bank, y2_bank, t3_bank = [PT, SA], [K0, SB_], [K1, SA], [SC, PY], [SD, SB_], [PT, SA]
        e_banks = [[K0, K1], [PT, SB_], [SC, SD], [SA, PY]]
        sum_bank = {2: SC, 3: SD}

        block = ctx.enter_context(nc.Block())

        def has(b, i, k):
            return not isinstance(b, int) or 0 <= GPB * b + i + k < NG

        def run_steps(eng, step):
            with eng.Fori(0, B - 1) as b:
                for i in range(GPB):
                    step(b, i)
            for i in range(GPB):
                step(B - 1, i)

        @block.sync
        def _(sp):
            sp.dma_start(xin[:], x.rearrange("b s d -> s b d")).then_inc(s_x, 16)
            sp.dma_start(w1[:], first).then_inc(s_w1, 16)
            src = ctx_x.rearrange("b (p j t) d -> j p b (t d)", p=P, j=GPB)

            def load(b, i):
                if isinstance(b, int) and b < 0:
                    pass
                else:
                    sp.wait_ge(s_z, (TG + 1) * (GPB * b + i + 1))
                sp.dma_start(xctx[:, i, :, :].rearrange("p t d -> p (t d)"),
                             src[i, :, bass.ds(b + 1, 1), :].rearrange("p b n -> p (b n)")).then_inc(s_ctx[i], 16)

            load(-1, 0)
            sp.dma_start(w1b[:], second).then_inc(s_w1b, 16)
            load(-1, 1)
            sp.dma_start(w2[:], later).then_inc(s_w2, 16)
            load(-1, 2)
            load(-1, 3)
            with sp.Fori(0, B - 1) as b:
                for i in range(GPB):
                    load(b, i)
            sp.dma_start(wexp[:], experts.rearrange("e d h -> d e h")).then_inc(s_exp_w, 16)
            for n in range(2):
                sp.wait_ge(s_t["acc"], 2 * n + 2)
                sp.dma_start(out[2 * n:2 * n + 2].rearrange("b s d -> s b d"), xmid[:, 2 * n:2 * n + 2, :])\
                    .then_inc(s_out, 16)
            sp.wait_ge(s_out, 32)

        @block.gpsimd
        def _(pool):
            pool.dma_start(mask8[:], mask.rearrange("b (p t) -> p b t", p=P)).then_inc(s_mask, 16)
            pool.wait_ge(s_w1, 16)
            for a in range(2):
                nc.gpsimd.tensor_copy(vo[:, a, :, P], ident[:, P - 1:P].to_broadcast([P, H])).then_inc(s_vo, 1)

            def step(b, i):
                if has(b, i, 4):
                    g4 = GPB * b + i + 4
                    pool.wait_ge(s_mask, 16)
                    pool.wait_ge(s_lns, g4 + 1)
                    if not (isinstance(b, int) and b < 0):
                        pool.wait_ge(s_PV, g4 + 1)
                    pool.sem_inc(s_slot, 1)
                    for t in range(TG):
                        nc.gpsimd.tensor_scalar(zt[:, i, t, 0:P - 1], xctx[:, i, t, 0:P - 1], rs[:, i % 2, t:t + 1],
                                                nm[:, i % 2, t:t + 1], ALU.mult, ALU.add).then_inc(s_z, 1)
                    nc.gpsimd.tensor_copy(zt[:, i, :, P - 1], mk[:, i % 2, :]).then_inc(s_z, 1)

            for i in range(GPB):
                step(-1, i)
            pool.wait_ge(s_x, 16)
            pool.wait_ge(s_bc, 32)
            nc.gpsimd.tensor_tensor(xres[:], xin[:], bc_["b_out"].rearrange("p (o d) -> p o d", o=1).to_broadcast([P, B, P]),
                                    ALU.add).then_inc(s_xres, 1)
            run_steps(pool, step)
            pool.wait_ge(s_bc, 32)
            for n, (lo, hi) in enumerate(PARTS):
                pool.wait_ge(s_t["res"], n + 1)
                nc.gpsimd.tensor_tensor(xmid[:, lo:hi, :], xres[:, lo:hi, :],
                                        bc_["b_o"].rearrange("p (o d) -> p o d", o=1).to_broadcast([P, hi - lo, P]),
                                        ALU.add).then_inc(s_t["bo"], 1)

        @block.scalar
        def _(act):
            act.preload_act_table_set("natural_log_exp_and_others")
            act.dma_start(bc[:], bcast.partition_broadcast(P)).then_inc(s_bc, 16)
            act.dma_start(row[:], rows).then_inc(s_bc, 16)

            def rsqrt_guess(src, mid, dst, ready, done, n):
                act.wait_ge(ready, n)
                nc.scalar.activation(mid, src, ACT.Ln).then_inc(done, 1)
                act.wait_ge(done, 2 * n - 1)
                nc.scalar.activation(dst, mid, ACT.Exp, scale=-0.5).then_inc(done, 1)

            def copy(dst, src, ready, n, done):
                act.wait_ge(ready, n)
                nc.scalar.copy(dst, src).then_inc(done, 1)

            def square(b, i):
                g = GPB * b + i
                act.wait_ge(s_K, g + 3)
                if not (isinstance(b, int) and g + 2 < 1):
                    act.wait_ge(s_nb, g + 4)
                nc.scalar.activation(ksq[:], pK[i % 2][:], ACT.Square).then_inc(s_Ksq, 1)

            def probabilities(b, i):
                g, k = GPB * b + i, (i + 1) % GPB
                act.wait_ge(s_S, g + 2)
                act.wait_ge(s_nr, g + 2)
                act.wait_ge(s_PV, g + 2)
                for n in range(TG * H):
                    last = nc.scalar.activation(prob[:, k, n // H, (n % H) * P:(n % H + 1) * P], pS[k % 2][:, n, :],
                                                ACT.Exp, bias=guard[:, 0:1], scale=nr[:, k % 2, n:n + 1])
                last.then_inc(s_P, 1)

            def group_rsqrt(b, i):
                n = GPB * b + i + 5
                lo, hi = (0 if has(b, i, 2) else 8), (12 if has(b, i, 4) else 8)
                act.wait_ge(s_nb, n)
                nc.scalar.activation(nl[:, lo:hi], nb[:, lo:hi], ACT.Ln).then_inc(s_ny, 1)
                act.wait_ge(s_ny, 2 * n - 1)
                nc.scalar.activation(ny[:, lo:hi], nl[:, lo:hi], ACT.Exp, scale=-0.5).then_inc(s_ny, 1)

            def transposed_copy(b, i):
                act.wait_ge(s_T, GPB * b + i + 4)
                nc.scalar.copy(zT[:, (i + 1) % 2], pT[:]).then_inc(s_Tc, 1)

            def batch_sums(b):
                act.wait_ge(s_PV, GPB * (b + 1) + GPB)
                nc.scalar.copy(y[:, 1].rearrange("p b h n -> p b (h n)")[:, bass.ds(b, 1), :]
                               .rearrange("p o n -> p (o n)"), pY[:, 0:H * P]).then_inc(s_Y, 1)

            def step(b, i):
                if has(b, i, 2):
                    square(b, i)
                if has(b, i, 1):
                    probabilities(b, i)
                if has(b, i, 2) or has(b, i, 4):
                    group_rsqrt(b, i)
                if isinstance(b, int) and b == B - 1 and i == GPB - 2:
                    for h in range(H):
                        copy(vo[:, :, h, 0:P], [SA, SB_][h][:, 0:2, :], s_pe0, 5, s_wcopy)
                if has(b, i, 0) and i == GPB - 1:
                    batch_sums(b)

            rsqrt_guess(qnb[:, 0:B], qnl[:, 0:B], qny[:, 0:B], s_lnin, s_lnout, 1)
            copy(wproj[:], SA[:, 0:3, :], s_pe0, 1, s_wcopy)
            copy(zlT[:], PY, s_lT, 1, s_lTc)
            group_rsqrt(-1, 0)
            for n in range(2):
                act.wait_ge(s_qk, n + 1)
                nc.scalar.activation(qksq[:, n, :], [SC, SD][n].rearrange("p b d -> p (b d)"), ACT.Square)\
                    .then_inc(s_qksq, 1)
            rsqrt_guess(qnb[:, 0:8], qnl[:, 0:8], qny[:, 0:8], s_qnb, s_qny, 1)
            act.wait_ge(s_pe0, 2)
            act.wait_ge(s_amat, 3)
            nc.scalar.activation(wT[:, 0], SB_[:, 0:2, :], ACT.Copy, scale=gcol[:, 0:1])
            copy(wT[:, 1], SB_[:, 2:4, :], s_pe0, 2, s_wcopy)
            transposed_copy(-1, 1)
            rsqrt_guess(qnb[:, 8:16], qnl[:, 8:16], qny[:, 8:16], s_qnb, s_qny, 2)
            copy(w2t[:], K1[:, 0:3, :], s_pe0, 3, s_wcopy)
            copy(qT[:], PY, s_qT, 1, s_qTc)
            copy(g2[:], K1[:, 0:2, :], s_pe0, 4, s_wcopy)
            square(-1, 2)
            for n in range(H):
                copy(qw[:, 1, :, n, :], [SA, SB_][n], s_qw, n + 1, s_qwc)
            group_rsqrt(-1, 1)
            for n in range(H):
                copy(qw[:, 0, :, n, :], [SC, SD][n], s_qw, n + 3, s_qwc)
            group_rsqrt(-1, 2)
            transposed_copy(-1, 2)
            act.wait_ge(s_guard, 1)
            probabilities(-1, 3)
            square(-1, 3)
            act.wait_ge(s_qnr, 2)
            for b in range(B):
                act.wait_ge(s_siml, b // 2 + 1)
                for h in range(H):
                    n = b * H + h
                    last = nc.scalar.activation(probl[:, b, h * P:(h + 1) * P], [PY, K0][b // 2][:, n % 4, :], ACT.Exp,
                                                bias=guard[:, 0:1], scale=qnr[:, 8 + n:9 + n])
                if b % 2:
                    last.then_inc(s_probl, 1)
                if b == 1:
                    group_rsqrt(-1, 3)
            transposed_copy(-1, 3)
            for n in range(2):
                copy(y[:, 0, 2 * n:2 * n + 2].rearrange("p b h n -> p (b h) n"), [PY, K0][n], s_yl, n + 1, s_ylc)

            run_steps(act, step)

            def part_rsqrt(ready, done, n):
                lo, hi = PARTS[n]
                rsqrt_guess(qnb[:, lo:hi], qnl[:, lo:hi], qny[:, lo:hi], s_t[ready], s_t[done], n + 1)

            def part_normalise(dst, offset, done, cols, n):
                act.wait_ge(s_t[offset], n + 1)
                for b in range(*PARTS[n]):
                    last = nc.scalar.activation(dst[:, b, 0:cols], xres[:, b, 0:cols], ACT.Identity,
                                                bias=stt[:, 4, b:b + 1], scale=qnr[:, b:b + 1])
                last.then_inc(s_t[done], 1)

            def part_copy(dst, src, ready, done, n):
                lo, hi = PARTS[n]
                copy(dst[:, lo:hi, :], src[n][:, lo:hi, :], s_t[ready], n + 1, s_t[done])

            part_rsqrt("var1", "rsq1", 0)
            part_normalise(zl, "off1", "z2", P - 1, 0)
            part_copy(zT2, t2_bank, "T2", "T2c", 0)
            part_rsqrt("var1", "rsq1", 1)
            part_copy(uT, u_bank, "u", "uc", 0)
            part_normalise(zl, "off1", "z2", P - 1, 1)
            part_copy(v2, v_bank, "v", "v2", 0)
            part_copy(zT2, t2_bank, "T2", "T2c", 1)
            part_copy(uT, u_bank, "u", "uc", 1)
            part_copy(v2, v_bank, "v", "v2", 1)
            part_rsqrt("var2", "rsq2", 0)
            part_normalise(xl3, "off2", "z3", P, 0)
            part_copy(zT3, t3_bank, "T3", "T3c", 0)
            part_rsqrt("var2", "rsq2", 1)
            part_normalise(xl3, "off2", "z3", P, 1)
            part_copy(zT3, t3_bank, "T3", "T3c", 1)
            act.wait_ge(s_t["dif"], 1)
            nc.scalar.activation(ex[:], dif[:], ACT.Exp).then_inc(s_t["exp"], 1)
            act.wait_ge(s_t["we"], 1)
            for b in (2, 3):
                act.wait_ge(s_t["e"], EXPERT_ORDER.index(b) + 1)
                for e in range(E):
                    nc.scalar.activation(wex[:, b - 2, e, :], e_banks[b][e // 4][:, e % 4, :], ACT.Copy,
                                         scale=we[:, b, e:e + 1]).then_inc(s_t["scaled"], 1)

        @block.tensor
        def _(pe):
            mm = nc.tensor.matmul

            pe.sem_inc(s_PV, GPB)
            pe.sem_inc(s_Y, 1)
            pe.wait_ge(s_warm, 1)
            for n in range(WARM):
                mm(pK[0][:], warm[:, 0:P], warm[:])
            pe.wait_ge(s_amat, 2)
            pe.wait_ge(s_w1, 16)
            mm(SA[:, 0, :], amat[:, 0, :], w1_["wq"])
            mm(SA[:, 1, :], amat[:, 0, :], w1_["wk"])
            mm(SA[:, 2, :], amat[:, 1, :], w1_["wk"]).then_inc(s_pe0, 1)
            pe.wait_ge(s_zl, 1)
            for b in range(B):
                last = nc.tensor.transpose(PY[:, b, :], zl[:, b, :], ident)
            last.then_inc(s_lT, 1)
            pe.wait_ge(s_wcopy, 1)
            pe.wait_ge(s_lTc, 1)
            for n in range(2):
                for b in range(B):
                    last = mm([SC, SD][n][:, b, :], zlT[:, b, :], wproj[:, n, :])
                last.then_inc(s_qk, 1)

            def transposes(b, i):
                g = GPB * b + i
                pe.wait_ge(s_z, (TG + 1) * (g + 4))
                if not (isinstance(b, int) and g + 3 < 1):
                    pe.wait_ge(s_Tc, g + 3)
                for t in range(TG):
                    last = nc.tensor.transpose(pT[:, t, :], zt[:, (i + 3) % GPB, t, :], ident)
                last.then_inc(s_T, 1)

            def keys(b, i):
                g, k = GPB * b + i, i % 2
                pe.wait_ge(s_Tc, g + 3)
                if not (isinstance(b, int) and g + 2 < 2):
                    pe.wait_ge(s_Ksq, g + 1)
                for t in range(TG):
                    last = mm(pK[k][:, t * P:(t + 1) * P], zT[:, k, t, :], wproj[:, 2, :])
                last.then_inc(s_K, 1)

            def scores(b, i):
                g, k = GPB * b + i, i % 2
                if not (isinstance(b, int) and g + 2 < 2):
                    pe.wait_ge(s_P, g + 1)
                q = qw[:, 1].rearrange("p b h n -> p b (h n)")[:, bass.ds(b + (i + 2) // GPB, 1), :]\
                    .rearrange("p o n -> p (o n)")
                for t in range(TG):
                    last = mm(pS[k][:, 2 * t:2 * t + 2, :].rearrange("p h n -> p (h n)"), zT[:, k, t, :], q)
                last.then_inc(s_S, 1)

            am = amat[:].rearrange("p a d -> p (a d)")
            mm(SB_[:, 0:2, :].rearrange("p a d -> p (a d)"), w1_["wk"], am)
            pe.wait_ge(s_w1b, 16)
            mm(SB_[:, 2:4, :].rearrange("p a d -> p (a d)"), w1_["wv"], am).then_inc(s_pe0, 1)
            pe.wait_ge(s_w2, 16)
            pe.wait_ge(s_bc, 32)
            for n, (w, o) in enumerate((("wkT", "bk"), ("wvT", "bv"), ("wqT", "bq"))):
                mm(K1[:, n, :], w2_[w], w1_["cent"], start=True, stop=False)
                last = mm(K1[:, n, :], row_[o], row_["e_last"], start=False, stop=True)
            last.then_inc(s_pe0, 1)
            transposes(-1, 1)
            pe.wait_ge(s_qg, 1)
            for b in range(B):
                last = nc.tensor.transpose(PY[:, b, :], qg[:, b, :], ident)
            last.then_inc(s_qT, 1)
            pe.wait_ge(s_wcopy, 3)
            mm(K1[:, 0, :], w2t[:, 2, :], w2t[:, 0, :])
            mm(K1[:, 1, :], w2t[:, 1, :], w2_["woT"]).then_inc(s_pe0, 1)
            keys(-1, 2)

            def query_weights(n):
                a, h = 1 - n // H, n % H
                r = slice(h * DH, (h + 1) * DH)
                mm([SA, SB_, SC, SD][n].rearrange("p b d -> p (b d)"), wT[r, 0, a, :],
                   qT[r, :, :].rearrange("p b d -> p (b d)")).then_inc(s_qw, 1)

            pe.wait_ge(s_qTc, 1)
            pe.wait_ge(s_wcopy, 2)
            pe.wait_ge(s_qksq, 2)
            for n in range(2 * H - 1):
                query_weights(n)
            pe.wait_ge(s_qwc, 2)
            scores(-1, 2)
            transposes(-1, 2)
            query_weights(2 * H - 1)
            pe.wait_ge(s_qwc, 4)
            pe.wait_ge(s_Ksq, 1)
            for b in range(B):
                last = mm([PY, K0][b // 2][:, 2 * (b % 2):2 * (b % 2) + 2, :].rearrange("p h n -> p (h n)"),
                          zlT[:, b, :], qw[:, 0, b].rearrange("p h n -> p (h n)"))
                if b % 2:
                    last.then_inc(s_siml, 1)
            pe.wait_ge(s_wcopy, 4)
            keys(-1, 3)
            scores(-1, 3)
            transposes(-1, 3)
            for n in range(2):
                pe.wait_ge(s_probl, n + 1)
                for b in range(2 * n, 2 * n + 2):
                    last = mm([PY, K0][n][:, 2 * (b % 2):2 * (b % 2) + 2, :].rearrange("p h n -> p (h n)"), zl[:, b, :],
                              probl[:, b, :])
                last.then_inc(s_yl, 1)
            pe.wait_ge(s_ylc, 2)

            def early_outputs():
                pe.wait_ge(s_Y, B)
                pe.wait_ge(s_Tc, NG)
                pe.wait_ge(s_Ksq, NG)
                pe.wait_ge(s_P, NG - 1)
                pe.wait_ge(s_vo, 2)
                for a in range(2):
                    for h in range(H):
                        r = slice(h * DH, (h + 1) * DH)
                        last = mm([SA, SB_][h][:, a, :], wT[r, 1, a, :], w1_["wout"][r, :])
                last.then_inc(s_pe0, 1)
                pe.wait_ge(s_wcopy, 6)
                for b in range(B - 1):
                    for h in range(H):
                        mm(o_at(b, h), y[:, 0, b, h, :], vo[:, 0, h, :], start=True, stop=False)
                        last = mm(o_at(b, h), y[:, 1, b, h, :], vo[:, 1, h, :], start=False, stop=True)
                    last.then_inc(s_t["o"], 1)
                for h in range(H):
                    mm(o_at(B - 1, h), y[:, 0, B - 1, h, :], vo[:, 0, h, :], start=True, stop=False)

            def step(b, i):
                g = GPB * b + i
                if has(b, i, 2):
                    keys(b, i)
                if has(b, i, 0):
                    pe.wait_ge(s_P, g + 1)
                    if i == 0:
                        pe.wait_ge(s_Y, b + 1)
                    for t in range(TG):
                        last = mm(pY[:, 0:H * P], zt[:, i, t, :], prob[:, i, t, :],
                                  start=(i == 0 and t == 0), stop=(i == GPB - 1 and t == TG - 1))
                    last.then_inc(s_PV, 1)
                if has(b, i, 3):
                    transposes(b, i)
                if has(b, i, 2):
                    scores(b, i)
                if isinstance(b, int) and b == B - 1 and i == GPB - 2:
                    early_outputs()

            run_steps(pe, step)

            pe.wait_ge(s_Y, B + 1)
            for h in range(H):
                last = mm(o_at(B - 1, h), y[:, 1, B - 1, h, :], vo[:, 1, h, :], start=False, stop=True)
            last.then_inc(s_t["o"], 1)
            for n, (lo, hi) in enumerate(PARTS):
                cols = slice(lo * P, hi * P)
                pe.wait_ge(s_t["z2"], n + 1)
                for b in range(lo, hi):
                    last = nc.tensor.transpose(t2_bank[n][:, b, :], zl[:, b, :], ident)
                last.then_inc(s_t["T2"], 1)
                pe.wait_ge(s_t["T2c"], n + 1)
                mm(u_bank[n][:, lo:hi, :].rearrange("p b s -> p (b s)"), g2[:, 0, :], zT2[:].rearrange("p b s -> p (b s)")[:, cols]).then_inc(s_t["u"], 1)
                for b in range(lo, hi):
                    last = mm(v_bank[n][:, b, :], zT2[:, b, :], g2[:, 1, :])
                last.then_inc(s_t["v"], 1)
                pe.wait_ge(s_t["uc"], n + 1)
                for b in range(lo, hi):
                    last = mm(s_bank[n][:, b, :], zT2[:, b, :], uT[:, b, :])
                last.then_inc(s_t["s"], 1)
            for n, (lo, hi) in enumerate(PARTS):
                pe.wait_ge(s_t["att"], n + 1)
                pe.wait_ge(s_t["v2"], n + 1)
                for b in range(lo, hi):
                    last = mm(y2_bank[n][:, b, :], att[:, b, :], v2[:, b, :])
                last.then_inc(s_t["y2"], 1)

            def experts_of(b):
                for k in range(2):
                    last = mm(e_banks[b][k].rearrange("p e h -> p (e h)"), zT3[:, b, :],
                              wexp[:, 4 * k:4 * k + 4, :].rearrange("p e h -> p (e h)"))
                last.then_inc(s_t["e"], 1)

            pe.wait_ge(s_exp_w, 16)
            for n, (lo, hi) in enumerate(PARTS):
                pe.wait_ge(s_t["z3"], n + 1)
                for b in range(lo, hi):
                    last = nc.tensor.transpose(t3_bank[n][:, b, :], xl3[:, b, :], ident)
                last.then_inc(s_t["T3"], 1)
                pe.wait_ge(s_t["T3c"], n + 1)
                for b in range(lo, hi):
                    last = mm(pY[:, b * E:(b + 1) * E], zT3[:, b, :], w2_["gate"])
                last.then_inc(s_t["logit"], 1)
                if n == 0:
                    experts_of(0)
                    experts_of(2)
            experts_of(1)
            pe.wait_ge(s_t["logc"], 1)
            experts_of(3)
            for b in (2, 3):
                for e in range(E):
                    n = E * (b - 2) + e + 1
                    pe.wait_ge(s_t["scaled"], max(n, 4) if b == 2 else n)
                    last = mm(sum_bank[b][:, 0, :], ident, wex[:, b - 2, e, :], start=e == 0, stop=e == E - 1)
                last.then_inc(s_t["sum"], 1)

        @block.vector
        def _(dve):
            v = nc.vector
            chain = [0]

            def mark(ins):
                chain[0] += 1
                ins.then_inc(dv, 1)
                return chain[0]

            def need(n):
                dve.wait_ge(dv, n)

            def link(ins):
                chain[0] += 1
                ins.then_inc(dv, 1)
                dve.wait_ge(dv, chain[0])

            def ln_terms(src, tmp, var, ln, factor=1.0, eps=LN_EPS):
                for t in range(TG):
                    last = v.bn_stats(bst[:, t, :], src[:, t, :])
                ln(last)
                v.tensor_tensor(tmp[:, 0], bst[:, :, 1], bst[:, :, 4], ALU.add)
                ln(v.tensor_tensor(tmp[:, 1], bst[:, :, 1], bst[:, :, 4], ALU.subtract))
                v.scalar_tensor_tensor(tmp[:, 2], bst[:, :, 2], eps / factor * P, bst[:, :, 5], ALU.add, ALU.add)
                ln(v.scalar_tensor_tensor(tmp[:, 3], tmp[:, 1], 0.25 * factor, tmp[:, 1], ALU.mult, ALU.mult))
                return v.scalar_tensor_tensor(var, tmp[:, 2], factor / P, tmp[:, 3], ALU.mult, ALU.add)

            def newton(val, guess, tmp, dst, ln):
                ln(v.tensor_tensor(tmp[:, 0], guess, guess, ALU.mult))
                ln(v.scalar_tensor_tensor(tmp[:, 1], tmp[:, 0], -0.5, val, ALU.mult, ALU.mult))
                return v.scalar_tensor_tensor(dst, tmp[:, 1], 1.5, guess, ALU.add, ALU.mult)

            v.memset(warm[:], 0.0).then_inc(s_warm, 1)
            v.memset(zl[:, :, P - 1], 1.0)

            dve.wait_ge(s_x, 16)
            ln_terms(xin, stt[:, 0:4], qnb[:, 0:B], link, 1 + LN_EPS, LN_EPS ** 2).then_inc(s_lnin, 1)

            dve.wait_ge(s_w1, 16)
            for a, n in ((1, "x"), (0, "l")):
                v.tensor_scalar(amat[:, a, 0:P - 1], w1_["cent"][:, 0:P - 1], w1_["g_" + n], None, ALU.mult)
                v.tensor_copy(amat[:, a, P - 1:P], w1_["b_" + n]).then_inc(s_amat, 1)
            v.scalar_tensor_tensor(gcol[:], w1_["g_q"], float(DH) ** 0.5, w1_["g_k"], ALU.mult, ALU.mult)\
                .then_inc(s_amat, 1)

            dve.wait_ge(s_lnin, 1)
            dve.wait_ge(s_lnout, 2)
            link(newton(qnb[:, 0:B], qny[:, 0:B], qnt[:, :, 0:B], qnr[:, 0:B], link))
            link(v.scalar_tensor_tensor(stt[:, 4], stt[:, 0], -0.5, qnr[:, 0:B], ALU.mult, ALU.mult))
            for b in range(B):
                last = v.tensor_scalar(zl[:, b, 0:P - 1], xin[:, b, 0:P - 1], qnr[:, b:b + 1], stt[:, 4, b:b + 1],
                                       ALU.mult, ALU.add)
            last.then_inc(s_zl, 1)
            dve.wait_ge(s_mask, 16)
            v.tensor_copy(maskf[:], mask8[:]).then_inc(s_maskf, 1)

            LINKS = 10
            base = {-4: chain[0]}

            def step(b, i):
                g = GPB * b + i
                n = [0]

                def ln(ins):
                    n[0] += 1
                    ins.then_inc(dv, 1)
                    before = base[-4] if first_step else base[-3] + LINKS * (g + 3)
                    dve.wait_ge(dv, before + n[0])

                lns, keys = has(b, i, 4), has(b, i, 2)
                first_step = isinstance(b, int) and g == -4
                if lns:
                    dve.wait_ge(s_ctx[i], 16 * (b + 2))
                    if not first_step:
                        dve.wait_ge(s_ny, 2 * (g + 4))
                    last = ln_terms(xctx[:, i], stt[:, 0:4], nb[:, 8:12], ln)
                    if not keys:
                        last.then_inc(s_nb, 1)
                    else:
                        ln(last)
                if keys:
                    dve.wait_ge(s_Ksq, g + 3)
                    ln(v.tensor_reduce(nb[:, 0:8], ksq[:].rearrange("p (n d) -> p n d", d=DH), AX.X, ALU.add))
                    v.tensor_scalar(nb[:, 0:8], nb[:, 0:8], SSQ_MIN, None, ALU.max).then_inc(s_nb, 1)
                if has(b, i, 3) and not (isinstance(b, int) and b < 0):
                    dve.wait_ge(s_T, g + 4)
                    v.tensor_copy(zT[:, (i + 1) % 2], pT[:]).then_inc(s_Tc, 1)
                if lns or keys:
                    lo, hi = (0 if keys else 8), (12 if lns else 8)
                    dve.wait_ge(s_ny, 2 * (g + 5))
                    dve.wait_ge(s_nb, g + 5)
                    if keys and not (isinstance(b, int) and g + 2 < 2):
                        dve.wait_ge(s_P, g + 1)
                    last = newton(nb[:, lo:hi], ny[:, lo:hi], nt[:, :, lo:hi], nr[:, i % 2, lo:hi], ln)
                    if keys:
                        last.then_inc(s_nr, 1)
                    if keys and lns:
                        dve.wait_ge(s_nr, g + 3)
                    elif lns:
                        ln(last)
                if lns:
                    dve.wait_ge(s_maskf, 1)
                    if not (isinstance(b, int) and g + 4 < 2):
                        dve.wait_ge(s_z, (TG + 1) * (g + 3))
                    mg = maskf[:, bass.ds(b + 1, 1), i * TG:(i + 1) * TG].rearrange("p o t -> p (o t)")
                    v.tensor_copy(mk[:, i % 2, :], mg)
                    ln(v.tensor_tensor(rs[:, i % 2, :], nr[:, i % 2, 8:12], mg, ALU.mult))
                    v.scalar_tensor_tensor(nm[:, i % 2, :], stt[:, 0], -0.5, rs[:, i % 2, :], ALU.mult, ALU.mult)\
                        .then_inc(s_lns, 1)
                assert n[0] <= LINKS
                dve.sem_inc(dv, LINKS - n[0])

            step(-1, 0)
            chain[0] += LINKS

            def sums_of_squares(n):
                dve.wait_ge(s_qksq, n + 1)
                q = qnb[:, 8 * n:8 * n + 8]
                link(v.tensor_reduce(q, qksq[:, n].rearrange("p (n d) -> p n d", d=DH), AX.X, ALU.add))
                v.tensor_scalar(q, q, SSQ_MIN, None, ALU.max).then_inc(s_qnb, 1)

            def norm_scales(n):
                dve.wait_ge(s_qnb, n + 1)
                dve.wait_ge(s_qny, 2 * n + 2)
                c = slice(8 * n, 8 * n + 8)
                newton(qnb[:, c], qny[:, c], qnt[:, :, c], qnr[:, c], link).then_inc(s_qnr, 1)

            sums_of_squares(0)
            norm_scales(0)
            dve.wait_ge(s_qnr, 1)
            v.tensor_tensor(qg[:].rearrange("p b (h d) -> p (b h) d", h=H), SC.rearrange("p b (h d) -> p (b h) d", h=H),
                            qnr[:, 0:8].rearrange("p (n o) -> p n o", o=1).to_broadcast([P, B * H, DH]), ALU.mult)\
                .then_inc(s_qg, 1)
            sums_of_squares(1)
            dve.wait_ge(s_bc, 32)
            link(v.tensor_tensor(gprod[:], bc_["q_gamma"], bc_["k_gamma"], ALU.mult))
            v.tensor_reduce(gmax[:, 0:1], gprod[:], AX.X, ALU.max)
            link(v.tensor_reduce(gmax[:, 1:2], gprod[:], AX.X, ALU.min))
            link(v.scalar_tensor_tensor(gmax[:, 0:1], gmax[:, 1:2], -1.0, gmax[:, 0:1], ALU.mult, ALU.max))
            link(v.tensor_scalar(gmax[:, 0:1], gmax[:, 0:1], -float(DH) ** 0.5, SIM_MAX, ALU.mult, ALU.add))
            v.tensor_scalar(guard[:], gmax[:, 0:1], 0.0, None, ALU.min).then_inc(s_guard, 1)
            norm_scales(1)
            base[-3] = chain[0]
            for i in range(1, GPB):
                step(-1, i)
            run_steps(dve, step)
            chain[0] += LINKS * (NG + 3)

            def residual(n):
                batches = range(*PARTS[n])
                count = {}
                for b in batches:
                    dve.wait_ge(s_t["o"], b + 1)
                    for h in range(H):
                        count[b, h] = mark(v.reciprocal(den[:, b, h:h + 1], o_at(b, h)[:, P:P + 1]))
                dve.wait_ge(s_xres, 1)
                for b in batches:
                    need(count[b, 1])
                    count[b] = mark(v.scalar_tensor_tensor(xmid[:, b, :], o_at(b, 0)[:, 0:P], den[:, b, 0:1],
                                                           xres[:, b, :], ALU.mult, ALU.add))
                for b in batches:
                    need(count[b])
                    last = v.scalar_tensor_tensor(xres[:, b, :], o_at(b, 1)[:, 0:P], den[:, b, 1:2], xmid[:, b, :],
                                                  ALU.mult, ALU.add)
                last.then_inc(s_t["res"], 1)
                dve.wait_ge(s_t["res"], n + 1)

            def layer_norm(k, n):
                lo, hi = PARTS[n]
                for b in range(lo, hi):
                    last = v.bn_stats(bst[:, b, :], xres[:, b, :])
                link(last)
                for b in range(lo, hi):
                    last = v.bn_aggr(mv[:, b, :], bst[:, b, :])
                link(last)
                v.tensor_scalar(qnb[:, lo:hi], mv[:, lo:hi, 1], LN_EPS, None, ALU.add).then_inc(s_t[f"var{k}"], 1)
                dve.wait_ge(s_t[f"var{k}"], n + 1)
                dve.wait_ge(s_t[f"rsq{k}"], 2 * n + 2)
                link(newton(qnb[:, lo:hi], qny[:, lo:hi], qnt[:, :, lo:hi], qnr[:, lo:hi], link))
                v.scalar_tensor_tensor(stt[:, 4, lo:hi], mv[:, lo:hi, 0], -1.0, qnr[:, lo:hi], ALU.mult, ALU.mult)\
                    .then_inc(s_t[f"off{k}"], 1)

            def attention_scores(n):
                lo, hi = PARTS[n]
                dve.wait_ge(s_t["s"], n + 1)
                v.tensor_tensor(att[:, lo:hi, :], s_bank[n][:, lo:hi, :],
                                w2_["decay"].rearrange("p (o d) -> p o d", o=1).to_broadcast([P, hi - lo, P]),
                                ALU.mult).then_inc(s_t["att"], 1)

            def second_residual(n):
                lo, hi = PARTS[n]
                dve.wait_ge(s_t["y2"], n + 1)
                dve.wait_ge(s_t["bo"], n + 1)
                dve.wait_ge(s_t["z2"], n + 1)
                link(v.tensor_tensor(xres[:, lo:hi, :], xmid[:, lo:hi, :], y2_bank[n][:, lo:hi, :], ALU.add))

            residual(0)
            layer_norm(1, 0)
            residual(1)
            layer_norm(1, 1)
            attention_scores(0)
            attention_scores(1)
            second_residual(0)
            layer_norm(2, 0)
            second_residual(1)
            layer_norm(2, 1)
            dve.wait_ge(s_t["logit"], 2)
            logit = pY[:, 0:B * E].rearrange("p (b e) -> p b e", b=B)
            count = [mark(v.max(top[:, b, :], logit[:, b, :])) for b in range(B)]
            for b in range(B):
                need(count[b])
                last = v.max_index(topi[:, b, :], top[:, b, :], logit[:, b, :])
            last.then_inc(s_t["logc"], 1)
            v.tensor_tensor(dif[:], top[:, :, 1], top[:, :, 0], ALU.subtract).then_inc(s_t["dif"], 1)
            dve.wait_ge(s_t["logc"], 1)
            link(v.tensor_copy(topf[:], topi[:, :, 0:2]))
            v.tensor_tensor(hot[:].rearrange("p b k e -> p (b k) e"),
                            bc_["iota"].rearrange("p (o e) -> p o e", o=1).to_broadcast([P, B * 2, E]),
                            topf[:].rearrange("p b (k o) -> p (b k) o", o=1).to_broadcast([P, B * 2, E]), ALU.is_equal)
            dve.wait_ge(s_t["exp"], 1)
            link(v.tensor_scalar(ex1[:], ex[:], 1.0, None, ALU.add))
            link(v.reciprocal(wt2[:, :, 0], ex1[:]))
            link(v.tensor_tensor(wt2[:, :, 1], ex[:], wt2[:, :, 0], ALU.mult))
            link(v.tensor_tensor(hotw[:].rearrange("p b k e -> p (b k) e"), hot[:].rearrange("p b k e -> p (b k) e"),
                                 wt2[:].rearrange("p b (k o) -> p (b k) o", o=1).to_broadcast([P, B * 2, E]), ALU.mult))
            v.tensor_tensor(we[:], hotw[:, :, 0, :], hotw[:, :, 1, :], ALU.add).then_inc(s_t["we"], 1)
            dve.wait_ge(s_t["we"], 1)
            dve.wait_ge(s_t["bo"], 2)
            dve.wait_ge(s_t["e"], EXPERT_ORDER.index(1) + 1)
            src = [xres[:, b, :] for b in range(2)]
            for e in range(E):
                for b in range(2):
                    if e > 0:
                        need(count[b])
                    dst = xmid[:, b, :] if e == E - 1 else acc[:, b, e % 2, :]
                    last = v.scalar_tensor_tensor(dst, e_banks[b][e // 4][:, e % 4, :], we[:, b, e:e + 1], src[b],
                                                  ALU.mult, ALU.add)
                    if e < E - 1:
                        count[b] = mark(last)
                    else:
                        last.then_inc(s_t["acc"], 1)
                    src[b] = dst
            for b in (2, 3):
                dve.wait_ge(s_t["sum"], b - 1)
                v.tensor_tensor(xmid[:, b, :], xres[:, b, :], sum_bank[b][:, 0, :], ALU.add).then_inc(s_t["acc"], 1)


def kernel(**inputs):
    import concourse.bacc as bacc
    from concourse.bass_utils import run_bass_kernel_spmd as run

    a = {k.replace("L0_", ""): np.ascontiguousarray(v) for k, v in inputs.items()}
    eye = np.eye(P, dtype=np.float32)
    cent = eye.copy()
    cent[P - 1, :] = -1.0
    cent[:, P - 1] = 0.0
    t = np.arange(P)
    lag = t[None, :] - 1 - t[:, None]
    decay = np.where(lag >= 0, LR * DECAY ** np.maximum(lag, 0).astype(np.float64), 0.0).astype(np.float32)
    e_last = eye[P - 1]
    wkv = a["xattn_W_kv"]
    first = np.concatenate([a["xattn_ln_l_g"][:, None], a["xattn_ln_l_b"][:, None], a["xattn_ln_x_g"][:, None],
                            a["xattn_ln_x_b"][:, None], np.tile(a["xattn_q_gamma"], H)[:, None],
                            np.tile(a["xattn_k_gamma"], H)[:, None], eye, cent, a["xattn_W_q"], wkv[:, :P]], axis=1)
    second = np.concatenate([wkv[:, P:], a["xattn_W_out"]], axis=1)
    later = np.concatenate([decay, a["attn_Wk"].T, a["attn_Wv"].T, a["attn_Wq"].T, a["attn_Wo"].T,
                            a["ffn_gate_w"].T], axis=1)
    rows = np.concatenate([a["attn_bk"], a["attn_bv"], a["attn_bq"], e_last])[None]
    bcast = np.concatenate([a["xattn_b_out"], a["attn_bo"], a["xattn_q_gamma"], a["xattn_k_gamma"],
                            np.arange(E, dtype=np.float32)])
    arrays = {"x": a["x"], "ctx": a["ctx_1024"], "mask": a["mask_BxS2_bk0"], "first": first, "second": second,
              "later": later, "rows": rows, "bcast": bcast, "experts": a["ffn_weight"]}
    arrays = {k: np.ascontiguousarray(v) for k, v in arrays.items()}
    nc = bacc.Bacc("TRN2", target_bir_lowering=False, num_devices=1)
    args = [nc.dram_tensor(k, v.shape, mybir.dt.from_np(v.dtype), kind="ExternalInput").ap() for k, v in arrays.items()]
    out = nc.dram_tensor("out", (B, P, P), F32, kind="ExternalOutput").ap()
    build(nc, *args, out)
    return run(nc, [arrays], core_ids=[0]).results[0]["out"]
```
